# Optimizing a Trainium2 kernel written in Bass

```python
import numpy as np
import jax
import jax.numpy as jnp

def _softmax(x, axis=-1):
    return jax.nn.softmax(x, axis=axis)

def _gelu(x):
    return jax.nn.gelu(x, approximate=True)

def _silu(x):
    return jax.nn.silu(x)

def _sigmoid(x):
    return jax.nn.sigmoid(x)

def _layernorm(x, axis=-1, eps=1e-05):
    m = jnp.mean(x, axis=axis, keepdims=True)
    v = jnp.var(x, axis=axis, keepdims=True)
    return (x - m) / jnp.sqrt(v + eps)

def _scatter_add(tgt, idx, src, axis=0):
    return tgt.at[idx].add(src)

def _segment_sum(src, seg, n):
    return jax.ops.segment_sum(src, seg, n)
kernel_name = 'mk_adaln_d1_jaxref_r8_e7967e'

def setup_inputs(seed: int=0):
    np.random.seed(seed)
    _w = jnp.asarray

    def _L0_attn_setup():
        import jax, jax.numpy as jnp
        import numpy as np
        key = jax.random.key(seed)
        ks = jax.random.split(key, 5)
        B, S, D = (1, 512, 256)
        H, Dh = (16, 128)
        scale = 1.0 / np.sqrt(D).astype(np.float32)
        return {'x': jax.random.normal(ks[0], (B, S, D), dtype=jnp.float32), 'W_K': jax.random.normal(ks[1], (H, Dh, D), dtype=jnp.float32) * scale, 'W_Q': jax.random.normal(ks[2], (H, Dh, D), dtype=jnp.float32) * scale, 'W_V': jax.random.normal(ks[3], (H, Dh, D), dtype=jnp.float32) * scale, 'W_O': jax.random.normal(ks[4], (D, H * Dh), dtype=jnp.float32) * scale}
    _L0_attn_in = _L0_attn_setup()

    def _L0_ffn_setup():
        import jax, jax.numpy as jnp
        import numpy as np
        COST_LAMBDA = 1e-07
        HID = [128, 256, 384, 512, 128, 256, 384, 512]
        TOP_K = 2

        def _gelu(v):
            return jax.nn.gelu(v, approximate=False)

        def _forward(x, down_w, down_b, up_w, up_b, router_w, router_b, shared_w1, shared_b1, shared_w2, shared_b2, core_w, core_b, expert_params):
            E = len(expert_params)
            h = x @ down_w + down_b
            cost = jnp.array([w1.shape[0] * w1.shape[1] + w2.shape[0] * w2.shape[1] for w1, _, w2, _ in expert_params], jnp.float32)
            logits = x @ router_w + router_b - COST_LAMBDA * cost
            probs = jax.nn.softmax(logits, axis=-1)
            topv, topi = jax.lax.top_k(probs, TOP_K)
            gate = jax.nn.softmax(topv, axis=-1)
            out = jnp.zeros_like(h)
            for k in range(TOP_K):
                mask = jax.nn.one_hot(topi[..., k], E, dtype=h.dtype)
                acc = jnp.zeros_like(h)
                for e, (w1, b1, w2, b2) in enumerate(expert_params):
                    hm = h * mask[..., e:e + 1]
                    acc = acc + (_gelu(_gelu(hm) @ w1 + b1) @ w2 + b2)
                out = out + acc * gate[..., k:k + 1]
            out = out + 0.1 * (_gelu(_gelu(h) @ shared_w1 + shared_b1) @ shared_w2 + shared_b2)
            out = out @ up_w + up_b
            out = out + (_gelu(x) @ core_w + core_b)
            return out
        key = jax.random.key(seed)
        ks = iter(jax.random.split(key, 80))

        def W(shape):
            return jax.random.normal(next(ks), shape, jnp.float32) * 0.02
        B, T, D, L = (4, 256, 256, 128)
        inp = {'x': jax.random.normal(next(ks), (B, T, D), jnp.float32)}
        inp['down_w'] = W((D, L))
        inp['down_b'] = jnp.zeros((L,), jnp.float32)
        inp['up_w'] = W((L, D))
        inp['up_b'] = jnp.zeros((D,), jnp.float32)
        inp['router_w'] = W((D, len(HID)))
        inp['router_b'] = jnp.zeros((len(HID),), jnp.float32)
        inp['shared_w1'] = W((L, L))
        inp['shared_b1'] = jnp.zeros((L,), jnp.float32)
        inp['shared_w2'] = W((L, L))
        inp['shared_b2'] = jnp.zeros((L,), jnp.float32)
        inp['core_w'] = W((D, D))
        inp['core_b'] = jnp.zeros((D,), jnp.float32)
        for e, h in enumerate(HID):
            inp[f'e{e}_w1'] = W((L, h))
            inp[f'e{e}_b1'] = jnp.zeros((h,), jnp.float32)
            inp[f'e{e}_w2'] = W((h, L))
            inp[f'e{e}_b2'] = jnp.zeros((L,), jnp.float32)
        return inp
    _L0_ffn_in = _L0_ffn_setup()
    _L0_c = _w((lambda *s: np.random.randn(*s).astype(np.float32) * 0.05)(4, 256))
    _L0_wmod = _w((lambda *s: np.random.randn(*s).astype(np.float32) * 0.05)(256, 6 * 256) * 256 ** (-0.5))
    _d = {'L0_attn_x': _L0_attn_in['x'], 'L0_attn_W_K': _L0_attn_in['W_K'], 'L0_attn_W_Q': _L0_attn_in['W_Q'], 'L0_attn_W_V': _L0_attn_in['W_V'], 'L0_attn_W_O': _L0_attn_in['W_O'], 'L0_ffn_down_w': _L0_ffn_in['down_w'], 'L0_ffn_down_b': _L0_ffn_in['down_b'], 'L0_ffn_up_w': _L0_ffn_in['up_w'], 'L0_ffn_up_b': _L0_ffn_in['up_b'], 'L0_ffn_router_w': _L0_ffn_in['router_w'], 'L0_ffn_router_b': _L0_ffn_in['router_b'], 'L0_ffn_shared_w1': _L0_ffn_in['shared_w1'], 'L0_ffn_shared_b1': _L0_ffn_in['shared_b1'], 'L0_ffn_shared_w2': _L0_ffn_in['shared_w2'], 'L0_ffn_shared_b2': _L0_ffn_in['shared_b2'], 'L0_ffn_core_w': _L0_ffn_in['core_w'], 'L0_ffn_core_b': _L0_ffn_in['core_b'], 'L0_ffn_e0_w1': _L0_ffn_in['e0_w1'], 'L0_ffn_e0_b1': _L0_ffn_in['e0_b1'], 'L0_ffn_e0_w2': _L0_ffn_in['e0_w2'], 'L0_ffn_e0_b2': _L0_ffn_in['e0_b2'], 'L0_ffn_e1_w1': _L0_ffn_in['e1_w1'], 'L0_ffn_e1_b1': _L0_ffn_in['e1_b1'], 'L0_ffn_e1_w2': _L0_ffn_in['e1_w2'], 'L0_ffn_e1_b2': _L0_ffn_in['e1_b2'], 'L0_ffn_e2_w1': _L0_ffn_in['e2_w1'], 'L0_ffn_e2_b1': _L0_ffn_in['e2_b1'], 'L0_ffn_e2_w2': _L0_ffn_in['e2_w2'], 'L0_ffn_e2_b2': _L0_ffn_in['e2_b2'], 'L0_ffn_e3_w1': _L0_ffn_in['e3_w1'], 'L0_ffn_e3_b1': _L0_ffn_in['e3_b1'], 'L0_ffn_e3_w2': _L0_ffn_in['e3_w2'], 'L0_ffn_e3_b2': _L0_ffn_in['e3_b2'], 'L0_ffn_e4_w1': _L0_ffn_in['e4_w1'], 'L0_ffn_e4_b1': _L0_ffn_in['e4_b1'], 'L0_ffn_e4_w2': _L0_ffn_in['e4_w2'], 'L0_ffn_e4_b2': _L0_ffn_in['e4_b2'], 'L0_ffn_e5_w1': _L0_ffn_in['e5_w1'], 'L0_ffn_e5_b1': _L0_ffn_in['e5_b1'], 'L0_ffn_e5_w2': _L0_ffn_in['e5_w2'], 'L0_ffn_e5_b2': _L0_ffn_in['e5_b2'], 'L0_ffn_e6_w1': _L0_ffn_in['e6_w1'], 'L0_ffn_e6_b1': _L0_ffn_in['e6_b1'], 'L0_ffn_e6_w2': _L0_ffn_in['e6_w2'], 'L0_ffn_e6_b2': _L0_ffn_in['e6_b2'], 'L0_ffn_e7_w1': _L0_ffn_in['e7_w1'], 'L0_ffn_e7_b1': _L0_ffn_in['e7_b1'], 'L0_ffn_e7_w2': _L0_ffn_in['e7_w2'], 'L0_ffn_e7_b2': _L0_ffn_in['e7_b2'], 'L0_c': _L0_c, 'L0_wmod': _L0_wmod}
    _x0 = _d['L0_attn_x']
    _d['L0_attn_x'] = jax.random.normal(jax.random.fold_in(jax.random.key(seed), 1), (4, 512, 256), dtype=_x0.dtype)
    del _x0
    return _d

def reference(L0_attn_x, L0_attn_W_K, L0_attn_W_Q, L0_attn_W_V, L0_attn_W_O, L0_ffn_down_w, L0_ffn_down_b, L0_ffn_up_w, L0_ffn_up_b, L0_ffn_router_w, L0_ffn_router_b, L0_ffn_shared_w1, L0_ffn_shared_b1, L0_ffn_shared_w2, L0_ffn_shared_b2, L0_ffn_core_w, L0_ffn_core_b, L0_ffn_e0_w1, L0_ffn_e0_b1, L0_ffn_e0_w2, L0_ffn_e0_b2, L0_ffn_e1_w1, L0_ffn_e1_b1, L0_ffn_e1_w2, L0_ffn_e1_b2, L0_ffn_e2_w1, L0_ffn_e2_b1, L0_ffn_e2_w2, L0_ffn_e2_b2, L0_ffn_e3_w1, L0_ffn_e3_b1, L0_ffn_e3_w2, L0_ffn_e3_b2, L0_ffn_e4_w1, L0_ffn_e4_b1, L0_ffn_e4_w2, L0_ffn_e4_b2, L0_ffn_e5_w1, L0_ffn_e5_b1, L0_ffn_e5_w2, L0_ffn_e5_b2, L0_ffn_e6_w1, L0_ffn_e6_b1, L0_ffn_e6_w2, L0_ffn_e6_b2, L0_ffn_e7_w1, L0_ffn_e7_b1, L0_ffn_e7_w2, L0_ffn_e7_b2, L0_c, L0_wmod):

    def _L0_attn_ref(x, W_K, W_Q, W_V, W_O):
        import jax, jax.numpy as jnp
        import numpy as np
        b, pos, d_model = x.shape
        d_head = W_K.shape[1]
        k = jnp.einsum('ihd,bpd->biph', W_K, x)
        q = jnp.einsum('ihd,bpd->biph', W_Q, x)
        v = jnp.einsum('ihd,bpd->biph', W_V, x)
        scores = jnp.einsum('biph,biqh->biqp', k, q)
        mask = jnp.tril(jnp.ones((pos, pos), dtype=x.dtype))
        masked = scores * mask - jnp.float32(10000000000.0) * (1.0 - mask)
        attn = jax.nn.softmax(masked / jnp.sqrt(jnp.float32(d_head)), axis=-1)
        z = jnp.einsum('biqp,biph->biqh', attn, v)
        z_flat = jnp.transpose(z, (0, 2, 1, 3)).reshape(b, pos, -1)
        out = jnp.einsum('df,bqf->bqd', W_O, z_flat)
        return out

    def _L0_ffn_ref(x, down_w, down_b, up_w, up_b, router_w, router_b, shared_w1, shared_b1, shared_w2, shared_b2, core_w, core_b, e0_w1, e0_b1, e0_w2, e0_b2, e1_w1, e1_b1, e1_w2, e1_b2, e2_w1, e2_b1, e2_w2, e2_b2, e3_w1, e3_b1, e3_w2, e3_b2, e4_w1, e4_b1, e4_w2, e4_b2, e5_w1, e5_b1, e5_w2, e5_b2, e6_w1, e6_b1, e6_w2, e6_b2, e7_w1, e7_b1, e7_w2, e7_b2):
        import jax, jax.numpy as jnp
        import numpy as np
        COST_LAMBDA = 1e-07
        HID = [128, 256, 384, 512, 128, 256, 384, 512]
        TOP_K = 2

        def _gelu(v):
            return jax.nn.gelu(v, approximate=False)

        def _forward(x, down_w, down_b, up_w, up_b, router_w, router_b, shared_w1, shared_b1, shared_w2, shared_b2, core_w, core_b, expert_params):
            E = len(expert_params)
            h = x @ down_w + down_b
            cost = jnp.array([w1.shape[0] * w1.shape[1] + w2.shape[0] * w2.shape[1] for w1, _, w2, _ in expert_params], jnp.float32)
            logits = x @ router_w + router_b - COST_LAMBDA * cost
            probs = jax.nn.softmax(logits, axis=-1)
            topv, topi = jax.lax.top_k(probs, TOP_K)
            gate = jax.nn.softmax(topv, axis=-1)
            out = jnp.zeros_like(h)
            for k in range(TOP_K):
                mask = jax.nn.one_hot(topi[..., k], E, dtype=h.dtype)
                acc = jnp.zeros_like(h)
                for e, (w1, b1, w2, b2) in enumerate(expert_params):
                    hm = h * mask[..., e:e + 1]
                    acc = acc + (_gelu(_gelu(hm) @ w1 + b1) @ w2 + b2)
                out = out + acc * gate[..., k:k + 1]
            out = out + 0.1 * (_gelu(_gelu(h) @ shared_w1 + shared_b1) @ shared_w2 + shared_b2)
            out = out @ up_w + up_b
            out = out + (_gelu(x) @ core_w + core_b)
            return out
        ep = [(e0_w1, e0_b1, e0_w2, e0_b2), (e1_w1, e1_b1, e1_w2, e1_b2), (e2_w1, e2_b1, e2_w2, e2_b2), (e3_w1, e3_b1, e3_w2, e3_b2), (e4_w1, e4_b1, e4_w2, e4_b2), (e5_w1, e5_b1, e5_w2, e5_b2), (e6_w1, e6_b1, e6_w2, e6_b2), (e7_w1, e7_b1, e7_w2, e7_b2)]
        return _forward(x, down_w, down_b, up_w, up_b, router_w, router_b, shared_w1, shared_b1, shared_w2, shared_b2, core_w, core_b, ep)
    x = L0_attn_x
    mod = (_silu(L0_c) @ L0_wmod).reshape(L0_c.shape[0], 6, 1, -1)
    sa, ca, ga, sb, cb, gb = (mod[:, 0], mod[:, 1], mod[:, 2], mod[:, 3], mod[:, 4], mod[:, 5])
    ga = (2 * (ga >= 0) - 1) * jnp.maximum(jnp.abs(ga), 0.25)
    gb = (2 * (gb >= 0) - 1) * jnp.maximum(jnp.abs(gb), 0.25)
    h = _layernorm(x, axis=-1) * (1 + ca) + sa
    x = x + ga * _L0_attn_ref(h, L0_attn_W_K, L0_attn_W_Q, L0_attn_W_V, L0_attn_W_O)
    h = _layernorm(x, axis=-1) * (1 + cb) + sb
    x = x + gb * _L0_ffn_ref(h, L0_ffn_down_w, L0_ffn_down_b, L0_ffn_up_w, L0_ffn_up_b, L0_ffn_router_w, L0_ffn_router_b, L0_ffn_shared_w1, L0_ffn_shared_b1, L0_ffn_shared_w2, L0_ffn_shared_b2, L0_ffn_core_w, L0_ffn_core_b, L0_ffn_e0_w1, L0_ffn_e0_b1, L0_ffn_e0_w2, L0_ffn_e0_b2, L0_ffn_e1_w1, L0_ffn_e1_b1, L0_ffn_e1_w2, L0_ffn_e1_b2, L0_ffn_e2_w1, L0_ffn_e2_b1, L0_ffn_e2_w2, L0_ffn_e2_b2, L0_ffn_e3_w1, L0_ffn_e3_b1, L0_ffn_e3_w2, L0_ffn_e3_b2, L0_ffn_e4_w1, L0_ffn_e4_b1, L0_ffn_e4_w2, L0_ffn_e4_b2, L0_ffn_e5_w1, L0_ffn_e5_b1, L0_ffn_e5_w2, L0_ffn_e5_b2, L0_ffn_e6_w1, L0_ffn_e6_b1, L0_ffn_e6_w2, L0_ffn_e6_b2, L0_ffn_e7_w1, L0_ffn_e7_b1, L0_ffn_e7_w2, L0_ffn_e7_b2)
    return x

_drawn_inputs = setup_inputs


def setup_inputs(seed=0):
    import zlib

    import numpy as np

    out = dict(_drawn_inputs(seed))
    spreads = {'L0_ffn_down_b': (0.0, 0.8),
     'L0_ffn_up_b': (0.0, 0.337),
     'L0_ffn_router_b': (0.0, 0.8),
     'L0_ffn_shared_b1': (0.0, 0.8),
     'L0_ffn_shared_b2': (0.0, 0.8),
     'L0_ffn_core_b': (0.0, 0.311),
     'L0_ffn_e0_b1': (0.0, 0.8),
     'L0_ffn_e0_b2': (0.0, 0.8),
     'L0_ffn_e1_b1': (0.0, 0.8),
     'L0_ffn_e1_b2': (0.0, 0.8),
     'L0_ffn_e2_b1': (0.0, 0.8),
     'L0_ffn_e2_b2': (0.0, 0.8),
     'L0_ffn_e3_b1': (0.0, 0.8),
     'L0_ffn_e3_b2': (0.0, 0.8),
     'L0_ffn_e4_b1': (0.0, 0.8),
     'L0_ffn_e4_b2': (0.0, 0.8),
     'L0_ffn_e5_b1': (0.0, 0.8),
     'L0_ffn_e5_b2': (0.0, 0.8),
     'L0_ffn_e6_b1': (0.0, 0.8),
     'L0_ffn_e6_b2': (0.0, 0.8),
     'L0_ffn_e7_b1': (0.0, 0.8),
     'L0_ffn_e7_b2': (0.0, 0.8)}
    factors = {'L0_ffn_down_w': 8.0,
     'L0_ffn_up_w': 3.494,
     'L0_ffn_router_w': 8.0,
     'L0_ffn_shared_w1': 8.0,
     'L0_ffn_shared_w2': 8.0,
     'L0_ffn_e0_w1': 8.0,
     'L0_ffn_e0_w2': 8.0,
     'L0_ffn_e1_w1': 8.0,
     'L0_ffn_e1_w2': 8.0,
     'L0_ffn_e2_w1': 8.0,
     'L0_ffn_e2_w2': 8.0,
     'L0_ffn_e3_w1': 8.0,
     'L0_ffn_e3_w2': 8.0,
     'L0_ffn_e4_w1': 8.0,
     'L0_ffn_e4_w2': 8.0,
     'L0_ffn_e5_w1': 8.0,
     'L0_ffn_e5_w2': 8.0,
     'L0_ffn_e6_w1': 8.0,
     'L0_ffn_e6_w2': 8.0,
     'L0_ffn_e7_w1': 8.0,
     'L0_ffn_e7_w2': 8.0}
    for name, (base, spread) in spreads.items():
        noise = np.random.default_rng([zlib.crc32(name.encode()), seed]).standard_normal(out[name].shape)
        drawn = base * np.exp(spread * noise) if base else spread * noise
        out[name] = jnp.asarray(drawn.astype(out[name].dtype))
    for name, factor in factors.items():
        out[name] = (out[name] * factor).astype(out[name].dtype)
    return out
```

```python
from contextlib import ExitStack

import concourse.bass as bass
from concourse import mybir

F32 = mybir.dt.float32
F32R = mybir.dt.float32r
U32 = mybir.dt.uint32
ALU = mybir.AluOpType
ACT = mybir.ActivationFunctionType
AX = mybir.AxisListType

B, S, D, H, DH = 4, 512, 256, 16, 128
NU = B * H
NG = 4
HID = [128, 256, 384, 512, 128, 256, 384, 512]
NC = sum(HID) // 128
EXPERT = [e for e, h in enumerate(HID) for _ in range(h // 128)]
INV = 1.0 / float(DH) ** 0.5
BIG = 3.0e38

F_W1, F_DOWN, F_CORE, F_SH1, F_SH2, F_UP, F_RT = 0, 2560, 2816, 3328, 3456, 3584, 3840
F_END = 3856
W2_END = NC * 128
C_ID, C_MASK, C_EXM, C_IOTA, C_COST, C_RB, C_ONE, C_END = 0, 128, 640, 800, 808, 816, 824, 832
B_DOWN, B_SH1, B_B1, B_END = 0, 1, 2, 22

P_OFF = [0, 128, 384, 768]
S_AT = [(1, 0), (2, 0), (1, 128), (0, 0)]
S_ORDER = [(2, [1]), (1, [0, 2]), (0, [3])]
T_OFF = [0, 512, 1024, 896]
T_AT = [(0, 0), (1, 0), (2, 0), (1, 384)]
T_COLS = [(0, 512), (512, 1024), (1024, 1280)]
T_ORDER = [(0, [0]), (1, [1, 3]), (2, [2])]


def unit(u):
    return u // 16, (u % 16) // 4, u % 4


def attention_plan():
    plan = [("mod",), ("wh", 0), ("wh", 1), ("lnp", 0), ("h", 0, 0), ("h", 0, 1), ("q", 0), ("k", 0), ("S", 0),
            ("wh", 2), ("v", 0, 0), ("v", 0, 1), ("q", 1), ("k", 1), ("norm", 0), ("v", 0, 2), ("v", 0, 3),
            ("T", 0), ("wh", 3)]
    ln1 = {0: ("lnp", 1), 3: ("lnp", 2), 6: ("lnp", 3)}
    h1 = {1: 1, 4: 2, 7: 3}
    for i in range(NU):
        if i + 1 < NU:
            plan.append(("S", i + 1))
        if i % 4 == 0 and i > 0:
            plan += [("wo", i // 4 - 1, 0), ("wo", i // 4 - 1, 1)]
        if i in h1:
            plan += [("h", h1[i], 0), ("h", h1[i], 1)]
        if i + 2 < NU:
            plan += [("q", i + 2), ("k", i + 2)]
        if i + 1 < NU:
            plan.append(("norm", i + 1))
        if i > 52 and i % 4 == 1:
            plan += [("h2", (i - 53) // 4, 0), ("h2", (i - 53) // 4, 1)]
        plan.append(("z", i))
        if i > 48 and i % 4 == 0:
            plan.append(("x2", (i - 52) // 4))
        if i > 52 and i % 4 == 2:
            plan += [("r", (i - 54) // 4)]
        if (i + 1) % 4 == 0 and i + 1 < NU:
            plan += [("v", (i + 1) // 4, c) for c in range(4)]
        if i in ln1:
            plan.append(ln1[i])
        if i < 48 and i % 16 in (5, 7, 9, 11):
            plan.append(("wh", 4 + 4 * (i // 16) + (i % 16 - 5) // 2))
        if 49 <= i < 53:
            plan.append(("wh", i - 33))
        if i == NU - 2:
            plan += [("wh", 20), ("wh", 21)]
        if i == NU - 1:
            plan += [("wh", 22)]
        if i + 1 < NU:
            plan.append(("T", i + 1))
    plan += [("wo", 15, 0), ("wo", 15, 1)]
    return plan


def ffn_plan():
    chunks = [(t, j) for t in range(B) for j in range(NC + 1)]
    at = {(0, 1): [("d0",), ("x2", 3)], (0, 5): [("h2", 3, 0), ("h2", 3, 1)], (0, 8): [("r", 3)],
          (0, 10): [("gx", 0)], (0, 12): [("dn", 1)], (0, 15): [("gx", 1)]}
    for t in range(1, B):
        at[t, 0] = [("D", t)]
        at[t, 4] = [("o", t - 1)]
        at[t, 6] = [("up", t - 1, 0), ("up", t - 1, 1)]
        if t + 1 < B:
            at[t, 10] = [("dn", t + 1)]
            at[t, 13] = [("gx", t + 1)]
    plan = [("dn", 0)]
    for n in range(len(chunks) + 2):
        if n < len(chunks):
            plan.append(("w1", n))
        plan += at.get(divmod(n, NC + 1), [])
        if n >= 2:
            plan.append(("w2", n - 2))
            if n == 2:
                plan += [("dt",), ("D", 0)]
            if EXP_OF(n - 2) != EXP_OF(n - 1):
                plan.append(("acc", *EXP_OF(n - 2)))
    plan += [("o", B - 1), ("up", B - 1, 0), ("up", B - 1, 1)]
    return plan


def EXP_OF(n):
    t, j = divmod(n, NC + 1)
    return t, (0 if j == 0 else 1 + EXPERT[j - 1])


MISC = {"h": True, "q": True, "k": True, "v": True, "z": True, "wo": False, "h2": True, "r": False,
        "dn": True, "o": True, "up": False}


def build(nc, x, ct, wmod, wat, wfa, wfb, cst, bcol, b2, ub, cb, sb2, out, scr):
    plan = attention_plan() + ffn_plan()
    use, rd = {}, {}
    for ev in plan:
        if ev[0] in MISC:
            use[ev] = len(use)
            if MISC[ev[0]]:
                rd[ev] = len(rd)
    accs = [ev for ev in plan if ev[0] in ("acc",)]
    acc_no = {ev[1:]: n for n, ev in enumerate(accs)}
    last_chunk = {}
    first_chunk = {}
    for n in range(B * (NC + 1)):
        last_chunk[EXP_OF(n)] = n
        first_chunk.setdefault(EXP_OF(n), n)

    wo_before = {}
    for ev in plan:
        if ev[0] in ("h", "h2"):
            wo_before[ev] = sum(1 for w in plan[:plan.index(ev)] if w[0] == "wo")

    with ExitStack() as ctx:
        def sb(name, cols, dt=F32, parts=128):
            return ctx.enter_context(nc.sbuf_tensor(name, [parts, cols], dt))

        def sem(name):
            return ctx.enter_context(nc.semaphore(name))

        hh, hl = sb("hh", 4096, F32R), sb("hl", 4096, F32R)
        W = [sb("W0", 8192, F32R), sb("W1", 8192, F32R)]
        vh, vl = sb("vh", 2048, F32R), sb("vl", 2048, F32R)
        qk = sb("qk", 2048, F32R)
        zt = sb("zt", 4096, F32R)
        pth, ptl = sb("pth", 1280, F32R), sb("ptl", 1280, F32R)
        g0z = sb("g0z", 320, F32R)
        X = sb("X", 4096)
        PB = sb("PB", 1280)
        tmp = sb("tmp", 1024)
        fb = sb("fb", 1024)
        stage = sb("stage", 2048)
        cc = sb("cc", C_END)
        gab = sb("gab", 2048)
        bc = sb("bc", B_END)
        rows = sb("rows", 1024, parts=8)
        oub = sb("oub", 256)
        ocb = sb("ocb", 128)
        modt = sb("modt", 32)
        sil = sb("sil", 24)
        mv = sb("mv", 8 + 24)
        rs = sb("rs", 32)
        sm = sb("sm", 4)
        nb = sb("nb", 4)
        ri = sb("ri", 4)
        wg = sb("wg", 128)
        rt = sb("rt", 256)
        ru = sb("ru", 32, U32)
        g0 = sb("g0", 20 + 160 + 8)
        Dm = sb("Dm", 128, parts=8)
        wT = sb("wT", 512, parts=8)

        PS = [ctx.enter_context(nc.psum_tensor(f"S{n}", [128, 512], F32)) for n in range(3)]
        PT = [ctx.enter_context(nc.psum_tensor(f"T{n}", [128, 512], F32)) for n in range(3)]
        M = [ctx.enter_context(nc.psum_tensor(f"M{n}", [128, 512], F32)) for n in range(2)]

        ident = cc[:, C_ID:C_ID + 128]
        mask = cc[:, C_MASK:C_MASK + 512]

        s_x = [sem(f"s_x{b}") for b in range(B)]
        s_ct, s_wm, s_c, s_b, s_g = sem("s_ct"), sem("s_wm"), sem("s_c"), sem("s_b"), sem("s_g")
        s_st = [sem("s_st0"), sem("s_st1")]
        s_wh, s_wl, s_wd = sem("s_wh"), sem("s_wl"), sem("s_wd")
        s_sil, s_mod, s_mc, s_gr, s_gd = sem("s_sil"), sem("s_mod"), sem("s_mc"), sem("s_gr"), sem("s_gd")
        mf, mh, me = sem("mf"), sem("mh"), sem("me")
        s_S, s_M, s_E, s_N, s_T = sem("s_S"), sem("s_M"), sem("s_E"), sem("s_N"), sem("s_T")
        s_ph, s_pl = sem("s_ph"), sem("s_pl")
        s_v, s_a = sem("s_v"), sem("s_a")
        s_ve, s_r0, s_xn = sem("s_ve"), sem("s_r0"), sem("s_xn")
        s_lg, s_le, s_wg = sem("s_lg"), sem("s_le"), sem("s_wg")
        s_f1, s_gh, s_gl, s_o, s_ac = sem("s_f1"), sem("s_gh"), sem("s_gl"), sem("s_o"), sem("s_ac")
        s_y = sem("s_y")
        s_hs, s_xg, s_xl = sem("s_hs"), sem("s_xg"), sem("s_xl")
        s_g0, s_gz, s_dt, s_dc, s_dd, s_dm = (sem(n) for n in ("s_g0", "s_gz", "s_dt", "s_dc", "s_dd", "s_dm"))
        s_wt, s_wc, s_D, s_Dc = sem("s_wt"), sem("s_wc"), sem("s_D"), sem("s_Dc")
        s_fin, s_out = sem("s_fin"), sem("s_out")

        def bank(ev):
            return M[use[ev] % 2]

        def hT(b, k):
            s = slice(b * 1024 + k * 512, b * 1024 + k * 512 + 512)
            return hh[:, s], hl[:, s]

        def hTc(b, k, c):
            s = slice(b * 1024 + k * 512 + c * 128, b * 1024 + k * 512 + c * 128 + 128)
            return hh[:, s], hl[:, s]

        def wt(slot, at, n):
            return W[slot][:, at:at + n], W[slot][:, 4096 + at:4096 + at + n]

        def zs(h):
            return zt[:, h * 1024:h * 1024 + 512], zt[:, h * 1024 + 512:h * 1024 + 1024]

        def u_at(t):
            o = (t % 2) * 1024
            return qk[:, o:o + 512], qk[:, o + 512:o + 1024]

        def gx_at(t, k):
            o = (t % 2) * 1024 + k * 512
            return vh[:, o:o + 512], vl[:, o:o + 512]

        def u32(t):
            return stage[:, 512:1024] if t else fb[:, 512:1024]

        def acc_at(t, c, n=128):
            return stage[:, 1024 + (t % 2) * 512 + 128 * c:1024 + (t % 2) * 512 + 128 * c + n]

        def lane(pair, a, n):
            return pair[0][:, a:a + n], pair[1][:, a:a + n]

        def piece(n):
            if n < 16:
                return wat[n // 4][:, (n % 4) * 1024:(n % 4) * 1024 + 1024], (n // 4) % 2, (n % 4) * 1024, 1024
            if n < 20:
                a = (n - 16) * 1024
                w = min(1024, F_END - a)
                return wfa[:, a:a + w], 0, a, w
            a = (n - 20) * 1024
            w = min(1024, W2_END - a)
            return wfb[:, a:a + w], 1, a, w

        def piece_after(n):
            if n < 8:
                return None
            if n < 20:
                return ("wo", n // 4 * 4 - 5, 1)
            return ("v", 15, 3)

        block = ctx.enter_context(nc.Block())

        @block.sync
        def _(sp):
            sp.dma_start(sil[:, 0:8], ct).then_inc(s_ct, 16)
            sp.dma_start(X[:, 0:1024], x[:, 0:1024]).then_inc(s_x[0], 16)
            sp.dma_start(cc[:], cst).then_inc(s_c, 16)
            for n in range(2):
                sp.dma_start(stage[:, n * 1024:n * 1024 + 1024], piece(n)[0]).then_inc(s_st[n], 16)
            for n in range(2, 23):
                if n == 4:
                    sp.wait_ge(s_mod, 2)
                    for b in range(1, B):
                        sp.dma_start(X[:, b * 1024:b * 1024 + 1024],
                                     x[:, b * 1024:b * 1024 + 1024]).then_inc(s_x[b], 16)
                if n < 4:
                    sp.wait_ge(s_wd, n - 1)
                else:
                    sp.wait_ge(s_wl, n - 3)
                src, _, _, w = piece(n)
                sp.dma_start(stage[:, (n % 2) * 1024:(n % 2) * 1024 + w], src).then_inc(s_st[n % 2], 16)
            for t in range(B):
                sp.wait_ge(s_fin, 2 * t + 2)
                sp.dma_start(out[:, t * 1024:t * 1024 + 1024], X[:, t * 1024:t * 1024 + 1024]).then_inc(s_out, 16)
            sp.wait_ge(s_out, 16 * B)

        @block.gpsimd
        def _(pool):
            pool.dma_start(bc[:], bcol).then_inc(s_b, 16)
            pool.dma_start(rows[:, 0:128], b2).then_inc(s_b, 16)
            pool.dma_start(oub[:], ub.broadcast_to([128, 256])).then_inc(s_b, 16)
            pool.dma_start(tmp[:, 0:256], cb.broadcast_to([128, 256])).then_inc(s_b, 16)
            pool.dma_start(ocb[:], sb2.broadcast_to([128, 128])).then_inc(s_b, 16)
            pool.wait_ge(s_gr, 1)
            pool.dma_start(scr, rows[0:4, 512:1024]).then_inc(s_gd, 16)
            pool.wait_ge(s_gd, 16)
            for b in range(B):
                pool.dma_start(gab[:, b * 512:b * 512 + 512],
                               scr[b:b + 1, :].broadcast_to([128, 512])).then_inc(s_g, 16)
            pool_chain = 0
            for ev in plan:
                if ev[0] == "wh" and ev[1] >= 2:
                    n = ev[1]
                    _, slot, a, w = piece(n)
                    hi, lo = wt(slot, a, w)
                    pool.wait_ge(s_wh, n + 1)
                    pool.tensor_tensor(lo, stage[:, (n % 2) * 1024:(n % 2) * 1024 + w], hi.bitcast(F32),
                                       ALU.subtract).then_inc(s_wl, 1)
                if ev[0] == "wo":
                    _, gb, c2 = ev
                    a = (gb % 4) * 1024 + c2 * 512
                    pool.wait_ge(me, use[ev] + 1)
                    if gb >= 4:
                        pool.wait_ge(s_y, 2 * gb + c2 - 7)
                    pool.tensor_tensor(X[:, a:a + 512], X[:, a:a + 512], fb[:, c2 * 512:c2 * 512 + 512],
                                       ALU.add).then_inc(s_y, 1)
                if ev[0] == "gx":
                    t = ev[1]
                    pool.wait_ge(me, use[("h2", t, 1)] + 1)
                    pool.wait_ge(s_wl, 21)
                    for k in range(2):
                        a, l = hT(t, k)
                        pool.wait_ge(s_xg, 2 * t + k)
                        pool.tensor_tensor(stage[:, 0:512], a.bitcast(F32), l.bitcast(F32),
                                           ALU.add).then_inc(s_hs, 1)
                if ev[0] == "up":
                    _, t, c = ev
                    f = fb[:, c * 512:c * 512 + 512].rearrange("p (a n) -> p a n", a=2)
                    g = gab[:, t * 512 + 256:t * 512 + 512].rearrange("p (a n) -> p a n", a=1)
                    y = X[:, t * 1024 + c * 512:t * 1024 + c * 512 + 512].rearrange("p (a n) -> p a n", a=2)
                    pool.wait_ge(me, use[ev] + 1)
                    pool.wait_ge(s_g, 64)
                    pool.tensor_tensor(f, f, g.broadcast_to([128, 2, 256]), ALU.mult).then_inc(s_a, 1)
                    pool_chain += 1
                    pool.wait_ge(s_a, pool_chain)
                    pool.tensor_tensor(y, y, f, ALU.add).then_inc(s_fin, 1)

        @block.scalar
        def _(act):
            act.dma_start(X[:, 1024:4096], wmod).then_inc(s_wm, 16)

            def rstd(n, base):
                act.wait_ge(s_ve, n + 1)
                act.activation(rs[:, base + 4:base + 8], rs[:, base:base + 4], ACT.Ln).then_inc(s_r0, 1)
                act.wait_ge(s_r0, 2 * n + 1)
                act.activation(rs[:, base + 8:base + 12], rs[:, base + 4:base + 8], ACT.Exp,
                               scale=-0.5).then_inc(s_r0, 1)

            ln_no = 0
            r_no = 0
            for ev in plan:
                kind = ev[0]
                if kind == "mod":
                    act.wait_ge(s_ct, 16)
                    act.activation(sil[:, 8:16], sil[:, 0:8], ACT.Exp, scale=-1.0).then_inc(s_sil, 1)
                elif kind == "wh":
                    n = ev[1]
                    _, slot, a, w = piece(n)
                    act.wait_ge(s_st[n % 2], 16 * (n // 2 + 1))
                    if piece_after(n):
                        act.wait_ge(mf, use[piece_after(n)] + 1)
                    act.copy(wt(slot, a, w)[0], stage[:, (n % 2) * 1024:(n % 2) * 1024 + w]).then_inc(s_wh, 1)
                elif kind in ("lnp", "x2"):
                    rstd(ln_no, 0 if ln_no % 2 == 0 else 16)
                    ln_no += 1
                elif kind in ("h", "h2"):
                    _, b, k = ev
                    o = 0 if kind == "h" else 16
                    act.wait_ge(mf, use[ev] + 1)
                    if use[ev] == 0:
                        act.wait_ge(s_mc, 1)
                    act.activation(hT(b, k)[0], bank(ev)[:], ACT.Identity,
                                   bias=modt[:, o + 4 * k + b:o + 4 * k + b + 1],
                                   scale=modt[:, o + 8 + 4 * k + b:o + 9 + 4 * k + b]).then_inc(mh, 1)
                elif kind in ("q", "k", "v", "z", "o"):
                    act.wait_ge(mf, use[ev] + 1)
                    if kind == "q":
                        dst = qk[:, 0:512]
                    elif kind == "k":
                        dst = qk[:, 1024:1536]
                    elif kind == "v":
                        dst = vh[:, ev[2] * 512:ev[2] * 512 + 512]
                    elif kind == "z":
                        dst = zs(ev[1] % 4)[0]
                    else:
                        dst = pth[:, 0:512]
                    act.copy(dst, bank(ev)[:]).then_inc(mh, 1)
                elif kind == "S":
                    u = ev[1]
                    for n, (bk, chunks) in enumerate(S_ORDER):
                        act.wait_ge(s_M, 3 * u + n + 1)
                        if u > 0 and n == 0:
                            act.wait_ge(s_N, u)
                        for i in chunks:
                            w = 128 * (i + 1)
                            a = S_AT[i][1]
                            ins = act.activation(PB[:, P_OFF[i]:P_OFF[i] + w], PS[bk][:, a:a + w], ACT.Exp,
                                                 bias=nb[:, i:i + 1], scale=-1.0, accum_out=sm[:, i:i + 1])
                        ins.then_inc(s_E, 1)
                elif kind == "T":
                    u = ev[1]
                    for n, (bk, _) in enumerate(T_ORDER):
                        a, z = T_COLS[bk]
                        act.wait_ge(s_T, 3 * u + n + 1)
                        act.copy(pth[:, a:z], PT[bk][:, 0:z - a]).then_inc(s_ph, 1)
                elif kind == "r":
                    act.wait_ge(s_lg, 2 * r_no + 1)
                    act.activation(rt[:, 64:96], rt[:, 32:64], ACT.Exp).then_inc(s_le, 1)
                    act.wait_ge(s_lg, 2 * r_no + 2)
                    act.activation(rt[:, 168:172], rt[:, 160:164], ACT.Exp).then_inc(s_le, 1)
                    r_no += 1
                elif kind == "d0":
                    act.wait_ge(s_b, 80)
                    act.activation(g0[:, 0:20], bc[:, B_B1:B_B1 + 20], ACT.Gelu).then_inc(s_g0, 1)
                elif kind == "dn":
                    t = ev[1]
                    act.wait_ge(mf, use[ev] + 1)
                    if t == 0:
                        act.wait_ge(s_b, 80)
                    if t == 0:
                        act.wait_ge(s_y, 32)
                    else:
                        act.wait_ge(s_xl, 2 * t)
                    act.activation(u32(t), bank(ev)[:], ACT.Gelu,
                                   bias=bc[:, B_DOWN:B_DOWN + 1]).then_inc(s_v, 1)
                    act.activation(u_at(t)[0], bank(ev)[:], ACT.Gelu,
                                   bias=bc[:, B_DOWN:B_DOWN + 1]).then_inc(mh, 1)
                elif kind == "gx":
                    t = ev[1]
                    act.wait_ge(me, use[("dn", t)] + 1)
                    if t >= 2:
                        act.wait_ge(mf, use[("up", t - 2, 1)] + 1)
                    for k in range(2):
                        act.wait_ge(s_hs, 2 * t + k + 1)
                        if k:
                            act.wait_ge(s_xl, 2 * t + 1)
                        act.activation(stage[:, 512:1024], stage[:, 0:512], ACT.Gelu).then_inc(s_v, 1)
                        act.activation(gx_at(t, k)[0], stage[:, 0:512], ACT.Gelu).then_inc(s_xg, 1)
                elif kind == "w1":
                    n = ev[1]
                    t, j = divmod(n, NC + 1)
                    bias = bc[:, B_SH1:B_SH1 + 1] if j == 0 else bc[:, B_B1 + j - 1:B_B1 + j]
                    act.wait_ge(s_f1, n + 1)
                    act.wait_ge(s_gl, n - 1) if n >= 2 else None
                    act.activation(PB[:, (n % 2) * 512:(n % 2) * 512 + 512], PS[n % 3][:], ACT.Gelu,
                                   bias=bias).then_inc(s_v, 1)
                    act.activation(zs(n % 4)[0], PS[n % 3][:], ACT.Gelu, bias=bias).then_inc(s_gh, 1)

        @block.tensor
        def _(pe):
            def mm3(o, lhs, rhs, start, stop, **kw):
                pe.matmul(o, lhs[0], rhs[0], start=start, stop=False, **kw)
                pe.matmul(o, lhs[0], rhs[1], start=False, stop=False, **kw)
                return pe.matmul(o, lhs[1], rhs[0], start=False, stop=stop, **kw)

            ln_no = 0
            for ev in plan:
                kind = ev[0]
                if kind in MISC:
                    m = use[ev]
                    o = bank(ev)
                    if m >= 2:
                        pe.wait_ge(me, m - 1)
                if kind == "mod":
                    pe.wait_ge(s_wm, 16)
                    pe.wait_ge(s_sil, 2)
                    wm = X[:, 1024:4096].rearrange("p (k n) -> p k n", k=2)
                    sl = sil[:, 16:24].rearrange("p (k n) -> p k n", k=2)
                    for n, j in enumerate((0, 1, 2, 3, 6, 7, 8, 9)):
                        for k in range(2):
                            ins = pe.matmul(PS[0][:, 4 * n:4 * n + 4], wm[:, k, 128 * j:128 * j + 128], sl[:, k, :],
                                            start=(k == 0), stop=(k == 1))
                    ins.then_inc(s_mod, 1)
                    for n, a in enumerate((512, 1280)):
                        for k in range(2):
                            ins = pe.matmul(PS[1][0:4, 256 * n:256 * n + 256], sl[:, k, :], wm[:, k, a:a + 256],
                                            start=(k == 0), stop=(k == 1))
                    ins.then_inc(s_mod, 1)
                elif kind in ("h", "h2"):
                    _, b, k = ev
                    if k == 0:
                        pe.wait_ge(s_xn, ln_no + 1)
                        ln_no += 1
                    if m == 0:
                        pe.wait_ge(s_c, 16)
                    for c in range(4):
                        ins = pe.transpose(o[:, 128 * c:128 * c + 128],
                                           tmp[:, 256 * c + 128 * k:256 * c + 128 * k + 128], ident)
                    ins.then_inc(mf, 1)
                elif kind in ("q", "k"):
                    g, b, h = unit(ev[1])
                    if h == 0:
                        pe.wait_ge(me, use[("h", b, 1)] + 1)
                        pc = 4 * g + (kind == "k")
                        pe.wait_ge(s_wd, pc + 1) if g == 0 else pe.wait_ge(s_wl, pc - 1)
                    a = (kind == "k") * 1024 + h * 128
                    for k in range(2):
                        ins = mm3(o[:], wt(g % 2, a + 512 * k, 128), hT(b, k), k == 0, k == 1)
                    ins.then_inc(mf, 1)
                elif kind == "v":
                    _, gb, c = ev
                    g, b = gb // 4, gb % 4
                    pe.wait_ge(s_wl, 4 * g + 1)
                    for k in range(2):
                        ins = mm3(o[:], hTc(b, k, c), wt(g % 2, 2048 + 512 * k, 512), k == 0, k == 1)
                    ins.then_inc(mf, 1)
                elif kind == "S":
                    u = ev[1]
                    pe.wait_ge(me, use[("k", u)] + 1)
                    if u == 0:
                        pe.wait_ge(s_mc, 1)
                        pe.wait_ge(s_gr, 1)
                    q = (qk[:, 0:512], qk[:, 512:1024])
                    kk = (qk[:, 1024:1536], qk[:, 1536:2048])
                    for n, (bk, chunks) in enumerate(S_ORDER):
                        if u > 0:
                            pe.wait_ge(s_E, 3 * u - 3 + n + 1)
                        for i in chunks:
                            a, w = S_AT[i][1], 128 * (i + 1)
                            ins = mm3(PS[bk][:, a:a + w], lane(q, 128 * i, 128), lane(kk, 0, w), True, True)
                        ins.then_inc(s_S, 1)
                elif kind == "T":
                    u = ev[1]
                    pe.wait_ge(s_N, u + 1)
                    for n, (bk, chunks) in enumerate(T_ORDER):
                        if u > 0:
                            pe.wait_ge(s_pl, 3 * u - 3 + n + 1)
                        for j in chunks:
                            a = T_AT[j][1]
                            for i in range(j, 4):
                                ins = pe.transpose(PT[bk][:, a + 128 * (i - j):a + 128 * (i - j) + 128],
                                                   PB[:, P_OFF[i] + 128 * j:P_OFF[i] + 128 * j + 128], ident)
                        ins.then_inc(s_T, 1)
                elif kind == "z":
                    u = ev[1]
                    h = u % 4
                    pe.wait_ge(me, use[("v", u // 4, 3)] + 1)
                    pe.wait_ge(s_pl, 3 * u + 3)
                    for j in range(4):
                        w = 512 - 128 * j
                        ins = mm3(o[:, 128 * j:512], (vh[:, 512 * j + 128 * h:512 * j + 128 * h + 128],
                                                      vl[:, 512 * j + 128 * h:512 * j + 128 * h + 128]),
                                  (pth[:, T_OFF[j]:T_OFF[j] + w], ptl[:, T_OFF[j]:T_OFF[j] + w]), j == 0, j == 3)
                    ins.then_inc(mf, 1)
                elif kind == "wo":
                    _, gb, c2 = ev
                    g = gb // 4
                    pe.wait_ge(me, use[("z", 4 * gb + 3)] + 1)
                    pe.wait_ge(s_wl, 4 * g + 2)
                    for c in range(2):
                        for h in range(4):
                            ins = mm3(o[:, 256 * c:256 * c + 256], lane(zs(h), 256 * c2 + 128 * c, 128),
                                      wt(g % 2, 3072 + 256 * h, 256), h == 0, h == 3)
                    ins.then_inc(mf, 1)
                elif kind == "r":
                    b = ev[1]
                    pe.wait_ge(s_wl, 18)
                    pe.wait_ge(me, use[("h2", b, 1)] + 1)
                    for c in range(4):
                        for k in range(2):
                            l, r = hTc(b, k, c), wt(0, F_RT + 8 * k, 8)
                            mm3(o[:, 8 * c:8 * c + 8], l, r, k == 0, False)
                            ins = pe.matmul(o[:, 8 * c:8 * c + 8], l[1], r[1], start=False, stop=(k == 1))
                    ins.then_inc(mf, 1)
                elif kind == "dn":
                    t = ev[1]
                    pe.wait_ge(s_wl, 18)
                    pe.wait_ge(me, use[("h2", t, 1)] + 1)
                    for k in range(2):
                        ins = mm3(o[:], wt(0, F_DOWN + 128 * k, 128), hT(t, k), k == 0, k == 1)
                    ins.then_inc(mf, 1)
                elif kind == "w1":
                    n = ev[1]
                    t, j = divmod(n, NC + 1)
                    if j == 0:
                        pe.wait_ge(me, use[("dn", t)] + 1)
                    if n >= 3:
                        pe.wait_ge(s_gh, n - 2)
                    else:
                        pe.wait_ge(s_E, 3 * NU)
                    a = F_SH1 if j == 0 else F_W1 + 128 * (j - 1)
                    mm3(PS[n % 3][:], wt(0, a, 128), u_at(t), True, True).then_inc(s_f1, 1)
                elif kind == "w2":
                    n = ev[1]
                    t, j = divmod(n, NC + 1)
                    X_ = acc_no[EXP_OF(n)]
                    first, last = first_chunk[EXP_OF(n)] == n, last_chunk[EXP_OF(n)] == n
                    pe.wait_ge(s_gl, n + 1)
                    if n == 0:
                        pe.wait_ge(s_pl, 3 * NU)
                    if n == 1:
                        pe.wait_ge(s_wl, 21)
                    if first and X_ >= 2:
                        pe.wait_ge(s_ac, X_ - 1)
                    w = wt(0, F_SH2, 128) if j == 0 else wt(1, 128 * (j - 1), 128)
                    for c in range(4):
                        ins = mm3(PT[X_ % 2][:, 128 * c:128 * c + 128], lane(zs(n % 4), 128 * c, 128), w,
                                  first and c == 0, last, skip_group_check=True)
                    if last:
                        ins.then_inc(s_o, 1)
                elif kind == "dt":
                    pe.wait_ge(s_wl, 21)
                    pe.wait_ge(s_gz, 1)
                    for c in range(NC):
                        w = wt(1, 128 * c, 128)
                        ins = mm3(PT[2][:, 0:8], w, (g0z[:, 8 * c:8 * c + 8], g0z[:, 160 + 8 * c:168 + 8 * c]),
                                  c == 0, c == NC - 1)
                    ins.then_inc(s_dt, 1)
                    pe.wait_ge(s_dc, 1)
                    pe.matmul(PT[2][0:8, 128:256], g0[:, 180:188], ident, start=True, stop=False)
                    pe.matmul(PT[2][0:8, 128:256], cc[0:8, C_ONE:C_ONE + 8], rows[0:8, 0:128],
                              start=False, stop=True).then_inc(s_dd, 1)
                elif kind == "D":
                    t = ev[1]
                    pe.wait_ge(s_wg, t + 1)
                    if t == 0:
                        pe.wait_ge(s_dm, 1)
                    else:
                        pe.wait_ge(s_Dc, t)
                    for c in range(4):
                        ins = pe.matmul(PT[2][0:8, 128 * c:128 * c + 128], wg[:, 32 * t + 8 * c:32 * t + 8 * c + 8],
                                        ident, start=True, stop=True)
                    ins.then_inc(s_wt, 1)
                    pe.wait_ge(s_wc, t + 1)
                    for c in range(4):
                        ins = pe.matmul(PT[2][:, 128 * c:128 * c + 128], wT[0:8, 128 * c:128 * c + 128], Dm[0:8, :],
                                        start=True, stop=True)
                    ins.then_inc(s_D, 1)
                elif kind == "o":
                    t = ev[1]
                    pe.wait_ge(s_ac, acc_no[(t, 8)] + 1)
                    for c in range(4):
                        ins = pe.transpose(o[:, 128 * c:128 * c + 128],
                                           acc_at(t, c), ident)
                    ins.then_inc(mf, 1)
                elif kind == "up":
                    _, t, c2 = ev
                    pe.wait_ge(me, use[("o", t)] + 1)
                    pe.wait_ge(s_xl, 2 * t + 2)
                    for c in range(2):
                        cx = 2 * c2 + c
                        oo = o[:, 256 * c:256 * c + 256]
                        mm3(oo, (pth[:, 128 * cx:128 * cx + 128], ptl[:, 128 * cx:128 * cx + 128]),
                            wt(0, F_UP, 256), True, False)
                        for k in range(2):
                            ins = mm3(oo, lane(gx_at(t, k), 128 * cx, 128), wt(0, F_CORE + 256 * k, 256),
                                      False, k == 1)
                    ins.then_inc(mf, 1)

        @block.vector
        def _(v):
            chain = [0]
            s_l = ctx.enter_context(nc.semaphore("s_l"))

            def link(ins):
                chain[0] += 1
                ins.then_inc(s_l, 1)
                v.wait_ge(s_l, chain[0])

            def bcast(ap, shape):
                return ap.broadcast_to(shape)

            def normal(n, src, parts=4):
                base = 0 if n % 2 == 0 else 16
                for c in range(parts):
                    ins = v.bn_stats(mv[:, 8 + 6 * c:14 + 6 * c], src[:, 256 * c:256 * c + 256])
                link(ins)
                for c in range(parts):
                    ins = v.bn_aggr(mv[:, 2 * c:2 * c + 2], mv[:, 8 + 6 * c:14 + 6 * c])
                link(ins)
                ve, r0, r = rs[:, base:base + 4], rs[:, base + 8:base + 12], rs[:, base + 12:base + 16]
                v.tensor_scalar(ve, mv[:, 1:8:2], 1e-5, None, ALU.add).then_inc(s_ve, 1)
                v.wait_ge(s_r0, 2 * n + 2)
                link(v.tensor_tensor(r, r0, r0, ALU.mult))
                link(v.tensor_tensor(r, r, ve, ALU.mult))
                link(v.tensor_scalar(r, r, -0.5, 1.5, ALU.mult, ALU.add))
                link(v.tensor_tensor(r, r, r0, ALU.mult))
                for c in range(parts):
                    ins = v.tensor_scalar(tmp[:, 256 * c:256 * c + 256], src[:, 256 * c:256 * c + 256],
                                          mv[:, 2 * c:2 * c + 1], r[:, c:c + 1], ALU.subtract, ALU.mult)
                ins.then_inc(s_xn, 1)

            ln_no = 0
            r_no = 0
            xv = 0
            for ev in plan:
                kind = ev[0]
                if kind == "mod":
                    v.wait_ge(s_b, 80)
                    link(v.tensor_tensor(oub[:], oub[:], tmp[:, 0:256], ALU.add))
                    v.tensor_scalar(ocb[:], ocb[:], 0.1, None, ALU.mult)
                    v.wait_ge(s_sil, 1)
                    link(v.tensor_scalar(sil[:, 16:24], sil[:, 8:16], 1.0, None, ALU.add))
                    link(v.reciprocal(sil[:, 16:24], sil[:, 16:24]))
                    v.tensor_tensor(sil[:, 16:24], sil[:, 16:24], sil[:, 0:8], ALU.mult).then_inc(s_sil, 1)
                    v.wait_ge(s_mod, 1)
                    link(v.tensor_copy(modt[:, 0:32], PS[0][:, 0:32]))
                    link(v.tensor_scalar(modt[:, 8:16], modt[:, 8:16], 1.0, None, ALU.add))
                    v.tensor_scalar(modt[:, 24:32], modt[:, 24:32], 1.0, None, ALU.add).then_inc(s_mc, 1)
                    v.wait_ge(s_mod, 2)
                    ra, rg = rows[0:4, 0:512], rows[0:4, 512:1024]
                    link(v.tensor_scalar(rg, PS[1][0:4, :], -1.0, 0.25, ALU.mult, ALU.max))
                    link(v.tensor_tensor(rg, PS[1][0:4, :], rg, ALU.max))
                    sg = PB[0:4, 0:512]
                    link(v.tensor_scalar(sg, PS[1][0:4, :], 0.0, 2.0, ALU.is_ge, ALU.mult))
                    v.scalar_tensor_tensor(out=rg, in0=sg, scalar=-1.0, in1=rg, op0=ALU.add,
                                           op1=ALU.mult).then_inc(s_gr, 1)
                elif kind == "wh" and ev[1] < 2:
                    n = ev[1]
                    _, slot, a, w = piece(n)
                    hi, lo = wt(slot, a, w)
                    v.wait_ge(s_wh, n + 1)
                    v.tensor_tensor(lo, stage[:, n * 1024:n * 1024 + w], hi.bitcast(F32), ALU.subtract)\
                     .then_inc(s_wd, 1)
                elif kind == "lnp":
                    b = ev[1]
                    v.wait_ge(s_x[b], 16)
                    if b:
                        v.wait_ge(mf, use[("h", b - 1, 1)] + 1)
                    normal(ln_no, X[:, b * 1024:b * 1024 + 1024])
                    ln_no += 1
                elif kind in ("h", "h2"):
                    _, b, k = ev
                    o = 0 if kind == "h" else 16
                    hi, lo = hT(b, k)
                    v.wait_ge(mh, rd[ev] + 1)
                    fbuf = fb[:, 512 * k:512 * k + 512]
                    v.wait_ge(s_y, wo_before[ev])
                    link(v.tensor_scalar(fbuf, bank(ev)[:], modt[:, o + 8 + 4 * k + b:o + 9 + 4 * k + b],
                                         modt[:, o + 4 * k + b:o + 4 * k + b + 1], ALU.mult, ALU.add))
                    v.tensor_tensor(lo, fbuf, hi.bitcast(F32), ALU.subtract).then_inc(me, 1)
                elif kind in ("q", "k", "v", "z", "o"):
                    v.wait_ge(mh, rd[ev] + 1)
                    if kind == "q":
                        hi, lo = qk[:, 0:512], qk[:, 512:1024]
                    elif kind == "k":
                        hi, lo = qk[:, 1024:1536], qk[:, 1536:2048]
                    elif kind == "v":
                        s = slice(ev[2] * 512, ev[2] * 512 + 512)
                        hi, lo = vh[:, s], vl[:, s]
                    elif kind == "z":
                        hi, lo = zs(ev[1] % 4)
                    else:
                        hi, lo = pth[:, 0:512], ptl[:, 0:512]
                    v.tensor_tensor(lo, bank(ev)[:], hi.bitcast(F32), ALU.subtract).then_inc(me, 1)
                elif kind == "S":
                    u = ev[1]
                    if u > 0:
                        v.wait_ge(s_E, 3 * u)
                    for n, (bk, chunks) in enumerate(S_ORDER):
                        v.wait_ge(s_S, 3 * u + n + 1)
                        for i in chunks:
                            a, w = S_AT[i][1], 128 * (i + 1)
                            ins = v.tensor_tensor_reduce(PS[bk][:, a:a + w], PS[bk][:, a:a + w],
                                                         mask[:, 512 - w:512], -INV, BIG, ALU.add, ALU.min,
                                                         nb[:, i:i + 1])
                        ins.then_inc(s_M, 1)
                elif kind == "norm":
                    u = ev[1]
                    v.wait_ge(s_E, 3 * u + 3)
                    link(v.reciprocal(ri[:], sm[:]))
                    for i in (1, 0, 2, 3):
                        p = PB[:, P_OFF[i]:P_OFF[i] + 128 * (i + 1)]
                        ins = v.tensor_scalar(p, p, ri[:, i:i + 1], None, ALU.mult)
                    ins.then_inc(s_N, 1)
                elif kind == "T":
                    u = ev[1]
                    for n, (bk, _) in enumerate(T_ORDER):
                        a, z = T_COLS[bk]
                        v.wait_ge(s_ph, 3 * u + n + 1)
                        v.tensor_tensor(ptl[:, a:z], PT[bk][:, 0:z - a], pth[:, a:z].bitcast(F32),
                                        ALU.subtract).then_inc(s_pl, 1)
                elif kind == "wo":
                    _, gb, c2 = ev
                    g, b = gb // 4, gb % 4
                    v.wait_ge(mf, use[ev] + 1)
                    v.wait_ge(s_y, 2 * gb + c2 - 1) if gb else None
                    if gb == 0:
                        v.wait_ge(s_g, 64)
                    ga = gab[:, b * 512:b * 512 + 256].rearrange("p (a n) -> p a n", a=1)
                    v.tensor_tensor(fb[:, c2 * 512:c2 * 512 + 512].rearrange("p (a n) -> p a n", a=2),
                                    bank(ev)[:].rearrange("p (a n) -> p a n", a=2), bcast(ga, [128, 2, 256]),
                                    ALU.mult).then_inc(me, 1)
                elif kind == "x2":
                    b = ev[1]
                    v.wait_ge(s_y, 2 * (12 + b) + 2)
                    v.wait_ge(mf, use[("h2", b - 1, 1) if b else ("h", 3, 1)] + 1)
                    normal(ln_no, X[:, b * 1024:b * 1024 + 1024])
                    ln_no += 1
                elif kind == "r":
                    b = ev[1]
                    v.wait_ge(mf, use[ev] + 1)
                    L = rt[:, 0:32]
                    L3 = L.rearrange("p (a n) -> p a n", a=4)
                    rb = cc[:, C_RB:C_RB + 8].rearrange("p (a n) -> p a n", a=1)
                    co = cc[:, C_COST:C_COST + 8].rearrange("p (a n) -> p a n", a=1)
                    io = cc[:, C_IOTA:C_IOTA + 8].rearrange("p (a n) -> p a n", a=1)
                    v.tensor_tensor(L3, bank(ev)[:, 0:32].rearrange("p (a n) -> p a n", a=4),
                                    bcast(rb, [128, 4, 8]), ALU.add).then_inc(me, 1)
                    v.wait_ge(me, use[ev] + 1)
                    link(v.tensor_tensor(L3, L3, bcast(co, [128, 4, 8]), ALU.subtract))
                    mx = rt[:, 96:100]

                    def per(ap):
                        return bcast(ap.rearrange("p (a n) -> p a n", n=1), [128, 4, 8])

                    link(v.tensor_reduce(mx, L3, AX.X, ALU.max))
                    e0 = rt[:, 32:64]
                    v.tensor_tensor(e0.rearrange("p (a n) -> p a n", a=4), L3, per(mx), ALU.subtract)\
                     .then_inc(s_lg, 1)
                    v.wait_ge(s_le, 2 * r_no + 1)
                    pr = rt[:, 64:96]
                    pr3 = pr.rearrange("p (a n) -> p a n", a=4)
                    link(v.tensor_reduce(mx, pr3, AX.X, ALU.add))
                    link(v.reciprocal(mx, mx))
                    link(v.tensor_tensor(pr3, pr3, per(mx), ALU.mult))
                    for c in range(4):
                        ins = v.max(rt[:, 128 + 8 * c:136 + 8 * c], pr[:, 8 * c:8 * c + 8])
                    link(ins)
                    for c in range(4):
                        ins = v.max_index(ru[:, 8 * c:8 * c + 8], rt[:, 128 + 8 * c:136 + 8 * c],
                                          pr[:, 8 * c:8 * c + 8])
                    link(ins)
                    idx = rt[:, 0:32]
                    link(v.tensor_copy(idx, ru[:]))
                    v.tensor_tensor(rt[:, 160:164], rt[:, 129:160:8], rt[:, 128:160:8], ALU.subtract)\
                     .then_inc(s_lg, 1)
                    v.wait_ge(s_le, 2 * r_no + 2)
                    ee, ga_, gb_ = rt[:, 168:172], rt[:, 172:176], rt[:, 176:180]
                    link(v.tensor_scalar(ga_, ee, 1.0, None, ALU.add))
                    link(v.reciprocal(ga_, ga_))
                    link(v.tensor_tensor(gb_, ga_, ee, ALU.mult))
                    a3 = rt[:, 32:64].rearrange("p (a n) -> p a n", a=4)
                    b3 = rt[:, 64:96].rearrange("p (a n) -> p a n", a=4)
                    io4 = bcast(io, [128, 4, 8])
                    v.tensor_tensor(a3, io4, per(idx[:, 0:32:8]), ALU.is_equal)
                    link(v.tensor_tensor(b3, io4, per(idx[:, 1:32:8]), ALU.is_equal))
                    v.tensor_tensor(a3, a3, per(ga_), ALU.mult)
                    link(v.tensor_tensor(b3, b3, per(gb_), ALU.mult))
                    v.tensor_tensor(wg[:, 32 * b:32 * b + 32].rearrange("p (a n) -> p a n", a=4), a3, b3, ALU.add)\
                     .then_inc(s_wg, 1)
                    v.wait_ge(s_wg, r_no + 1)
                    r_no += 1
                elif kind == "d0":
                    v.wait_ge(s_g0, 1)
                    gz = g0[:, 20:180]
                    a = g0[:, 0:20].rearrange("p (a n) -> p a n", n=1)
                    ex = cc[:, C_EXM:C_EXM + 160].rearrange("p (a n) -> p a n", n=8)
                    link(v.tensor_tensor(gz.rearrange("p (a n) -> p a n", n=8), ex, bcast(a, [128, 20, 8]), ALU.mult))
                    link(v.tensor_copy(g0z[:, 0:160], gz))
                    v.tensor_tensor(g0z[:, 160:320], gz, g0z[:, 0:160].bitcast(F32), ALU.subtract).then_inc(s_gz, 1)
                elif kind == "dt":
                    v.wait_ge(s_dt, 1)
                    v.tensor_copy(g0[:, 180:188], PT[2][:, 0:8]).then_inc(s_dc, 1)
                    v.wait_ge(s_dd, 1)
                    v.tensor_copy(Dm[0:8, :], PT[2][0:8, 128:256]).then_inc(s_dm, 1)
                elif kind == "D":
                    t = ev[1]
                    v.wait_ge(s_wt, t + 1)
                    v.tensor_copy(wT[0:8, :], PT[2][0:8, :]).then_inc(s_wc, 1)
                    v.wait_ge(s_D, t + 1)
                    if t == 0:
                        v.wait_ge(s_wl, 21)
                    if t >= 2:
                        v.wait_ge(mf, use[("o", t - 2)] + 1)
                    a = acc_at(t, 0, 512).rearrange("p (a n) -> p a n", a=4)
                    sbb = ocb[:].rearrange("p (a n) -> p a n", a=1)
                    v.tensor_tensor(a, PT[2][:].rearrange("p (a n) -> p a n", a=4), bcast(sbb, [128, 4, 128]),
                                    ALU.add).then_inc(s_Dc, 1)
                elif kind == "acc":
                    _, t, e = ev
                    n = acc_no[(t, e)]
                    v.wait_ge(s_o, n + 1)
                    v.wait_ge(s_Dc, t + 1)
                    v.wait_ge(s_ac, n) if n else None
                    for c in range(4):
                        a = acc_at(t, c)
                        sc = 0.1 if e == 0 else wg[:, 32 * t + 8 * c + e - 1:32 * t + 8 * c + e]
                        ins = v.scalar_tensor_tensor(out=a, in0=PT[n % 2][:, 128 * c:128 * c + 128], scalar=sc,
                                                     in1=a, op0=ALU.mult, op1=ALU.add)
                    ins.then_inc(s_ac, 1)
                elif kind == "dn":
                    v.wait_ge(mh, rd[ev] + 1)
                    xv += 1
                    v.wait_ge(s_v, xv)
                    hi, lo = u_at(ev[1])
                    v.tensor_tensor(lo, u32(ev[1]), hi.bitcast(F32), ALU.subtract).then_inc(me, 1)
                elif kind == "gx":
                    t = ev[1]
                    for k in range(2):
                        xv += 1
                        v.wait_ge(s_xg, 2 * t + k + 1)
                        v.wait_ge(s_v, xv)
                        hi, lo = gx_at(t, k)
                        v.tensor_tensor(lo, stage[:, 512:1024], hi.bitcast(F32), ALU.subtract).then_inc(s_xl, 1)
                elif kind == "w1":
                    n = ev[1]
                    xv += 1
                    v.wait_ge(s_gh, n + 1)
                    v.wait_ge(s_v, xv)
                    hi, lo = zs(n % 4)
                    v.tensor_tensor(lo, PB[:, (n % 2) * 512:(n % 2) * 512 + 512], hi.bitcast(F32),
                                    ALU.subtract).then_inc(s_gl, 1)
                elif kind == "up":
                    _, t, c2 = ev
                    v.wait_ge(mf, use[ev] + 1)
                    if t:
                        v.wait_ge(s_fin, 2 * t - 1 + c2)
                    f = fb[:, 512 * c2:512 * c2 + 512].rearrange("p (a n) -> p a n", a=2)
                    ob = oub[:].rearrange("p (a n) -> p a n", a=1)
                    v.tensor_tensor(f, bank(ev)[:].rearrange("p (a n) -> p a n", a=2), bcast(ob, [128, 2, 256]),
                                    ALU.add).then_inc(me, 1)


def kernel(**inputs):
    import numpy as np
    import concourse.bacc as bacc
    from concourse.bass_utils import run_bass_kernel_spmd

    A = {k: np.asarray(v) for k, v in inputs.items()}
    f = "L0_ffn_"

    def rowsplit(w):
        k = w.shape[0] // 128
        return w.reshape(k, 128, -1).transpose(1, 0, 2).reshape(128, -1)

    def perhead(w):
        return w.reshape(4, 4, 128, 2, 128).transpose(0, 4, 3, 1, 2).reshape(4, 128, 1024)

    wo = A["L0_attn_W_O"].reshape(256, 4, 4, 128).transpose(1, 3, 2, 0).reshape(4, 128, 1024)
    wat = np.concatenate([perhead(A["L0_attn_W_Q"]), perhead(A["L0_attn_W_K"]), perhead(A["L0_attn_W_V"]), wo], 2)
    wfa = np.concatenate([A[f"{f}e{e}_w1"] for e in range(8)] +
                         [rowsplit(A[f + "down_w"]), rowsplit(A[f + "core_w"]), A[f + "shared_w1"],
                          A[f + "shared_w2"], A[f + "up_w"], rowsplit(A[f + "router_w"])], 1)
    wfb = np.concatenate([rowsplit(A[f"{f}e{e}_w2"]) for e in range(8)], 1)
    b1 = np.concatenate([A[f"{f}e{e}_b1"].reshape(-1, 128).T for e in range(8)], 1)
    bcol = np.concatenate([A[f + "down_b"][:, None], A[f + "shared_b1"][:, None], b1], 1)
    b2 = np.stack([A[f"{f}e{e}_b2"] for e in range(8)])
    cst = np.zeros((128, C_END), np.float32)
    cst[:, C_ID:C_ID + 128] = np.eye(128)
    cst[:, C_MASK + 384:C_MASK + 512] = np.where(np.tril(np.ones((128, 128))) > 0, 0, -1e10)
    for c, e in enumerate(EXPERT):
        cst[:, C_EXM + 8 * c:C_EXM + 8 * c + 8] = np.arange(8) != e
    cst[:, C_IOTA:C_IOTA + 8] = np.arange(8)
    cst[:, C_COST:C_COST + 8] = np.float32(1e-7) * (np.array(HID, np.float32) * 256)
    cst[:, C_ONE:C_ONE + 8] = 1
    cst[:, C_RB:C_RB + 8] = A[f + "router_b"][None]
    ins = {
        "x": rowsplit(A["L0_attn_x"].reshape(2048, 256)),
        "ct": rowsplit(np.ascontiguousarray(A["L0_c"].T)),
        "wmod": rowsplit(A["L0_wmod"]),
        "wat": wat, "wfa": wfa, "wfb": wfb, "cst": cst, "bcol": bcol, "b2": b2,
        "ub": A[f + "up_b"][None], "cb": A[f + "core_b"][None], "sb2": A[f + "shared_b2"][None],
    }
    nc = bacc.Bacc("TRN2", target_bir_lowering=False, num_devices=1)
    arrays, aps = {}, {}
    for name, a in ins.items():
        arrays["in_" + name] = np.ascontiguousarray(a)
        aps[name] = nc.dram_tensor("in_" + name, a.shape, F32, kind="ExternalInput").ap()
    out = nc.dram_tensor("out_0", (128, 4096), F32, kind="ExternalOutput").ap()
    scr = nc.dram_tensor("scr", (4, 512), F32, kind="Internal").ap()
    build(nc, **aps, out=out, scr=scr)
    r = run_bass_kernel_spmd(nc, [arrays], core_ids=[0])
    y = np.asarray(r.results[0]["out_0"])
    return y.reshape(128, 16, 256).transpose(1, 0, 2).reshape(4, 512, 256)
```

```python
from contextlib import ExitStack

import concourse.bass as bass
from concourse import mybir

F32 = mybir.dt.float32
F32R = mybir.dt.float32r
U32 = mybir.dt.uint32
ALU = mybir.AluOpType
ACT = mybir.ActivationFunctionType
AX = mybir.AxisListType

B, S, D, H, DH = 4, 512, 256, 16, 128
NU = B * H
NG = 4
HID = [128, 256, 384, 512, 128, 256, 384, 512]
NC = sum(HID) // 128
EXPERT = [e for e, h in enumerate(HID) for _ in range(h // 128)]
INV = 1.0 / float(DH) ** 0.5
BIG = 3.0e38

F_W1, F_DOWN, F_CORE, F_SH1, F_SH2, F_UP, F_RT = 0, 2560, 2816, 3328, 3456, 3584, 3840
F_END = 3856
W2_END = NC * 128
C_ID, C_MASK, C_EXM, C_IOTA, C_COST, C_RB, C_ONE, C_END = 0, 128, 640, 800, 808, 816, 824, 832
B_DOWN, B_SH1, B_B1, B_SH2, B_END = 0, 1, 2, 22, 23

P_OFF = [0, 128, 384, 768]
S_AT = [(1, 0), (2, 256), (1, 128), (0, 0)]
S_ORDER = [(1, [0, 2]), (0, [3]), (2, [1])]
T_OFF = [0, 512, 1024, 896]
T_AT = [0, 0, 0, 384]
T_COLS = {0: (0, 512), 1: (512, 1024), 2: (1024, 1280)}
T_ORDER = [(2, [2]), (1, [1, 3]), (0, [0])]


def unit(u):
    return u // 16, (u % 16) // 4, u % 4


def attention_plan():
    at = {}

    def put(i, *events):
        at.setdefault(i, []).extend(events)

    for b in (1, 2, 3):
        put(3 * b - 3, ("lnp", b))
        put(3 * b - 2, ("h", b, 0), ("h", b, 1))
    for n in range(4, 16):
        put(16 * (n // 4 - 1) + 5 + 2 * (n % 4), ("wh", n))
    for n in range(16, 20):
        put(34 + n, ("wh", n))
    for b in range(3):
        put(53 + 4 * b, ("x2", b))
        put(54 + 4 * b, ("h2", b, 0), ("h2", b, 1))
        put(55 + 4 * b, ("r", b))
    put(57, ("wt", 0))
    put(61, ("wt", 1))
    put(62, ("wh", 20), ("wh", 21))
    put(63, ("wh", 22))
    plan = [("lnp", 0), ("mod",), ("h", 0, 0), ("h", 0, 1), ("wh", 0), ("wh", 1), ("q", 0), ("k", 0), ("mod2",),
            ("S", 0), ("wh", 2), ("q", 1), ("k", 1), ("norm", 0), ("v", 0, 0), ("v", 0, 1), ("T", 0), ("wh", 3)]
    for i in range(NU):
        if i + 1 < NU:
            plan.append(("S", i + 1))
        if i + 2 < NU:
            plan += [("q", i + 2), ("k", i + 2)]
        if i + 1 < NU:
            plan.append(("norm", i + 1))
        if i >= 2:
            plan.append(("wo", i // 2 - 1, i % 2))
        plan.append(("z", i))
        if i + 2 < NU:
            plan.append(("v", i // 2 + 1, i % 2))
        plan += at.get(i, [])
        if i + 1 < NU:
            plan.append(("T", i + 1))
    plan += [("wo", NU // 2 - 1, 0), ("wo", NU // 2 - 1, 1)]
    return plan


def ffn_plan():
    chunks = [(t, j) for t in range(B) for j in range(NC + 1)]
    at = {(0, 1): [("x2", 3), ("dt",), ("D", 0)], (0, 4): [("h2", 3, 0), ("h2", 3, 1)],
          (0, 8): [("r", 3)],
          (0, 10): [("gx", 0)], (0, 12): [("dn", 1)], (0, 14): [("wt", 2)], (0, 16): [("gx", 1)]}
    for t in range(1, B):
        at[t, 1] = [("D", t)]
        at[t, 3] = [("o", t - 1)]
        at[t, 5] = [("up", t - 1, 0)]
        at[t, 7] = [("up", t - 1, 1)]
        if t + 1 < B:
            at[t, 10] = [("dn", t + 1)]
            at[t, 13] = [("gx", t + 1)]
    at[1, 9] = [("wt", 3)]
    plan = [("wl", 0), ("wl", 1), ("d0",), ("dn", 0)]
    waiting = []
    for n in range(len(chunks) + 2):
        if n < len(chunks):
            plan.append(("w1", n))
        if n >= 2:
            plan.append(("w2", n - 2))
        for ev in at.get(divmod(n, NC + 1), []):
            plan.append(ev)
            if ev == ("h2", 3, 1):
                plan += [("wl", 2), ("wl", 3)]
            if ev[0] == "D":
                plan += [x for acc in waiting for x in acc]
                waiting = []
        if n >= 2 and EXP_OF(n - 2) != EXP_OF(n - 1):
            t, e = EXP_OF(n - 2)
            acc = [("acc", t, e)]
            if e and 8 * t + e + 3 < 8 * B:
                acc.append(("wl", 8 * t + e + 3))
            if ("D", t) in plan:
                plan += acc
            else:
                waiting.append(acc)
    plan += [("o", B - 1), ("up", B - 1, 0), ("up", B - 1, 1)]
    return plan


def EXP_OF(n):
    t, j = divmod(n, NC + 1)
    return t, (0 if j == 0 else 1 + EXPERT[j - 1])


MISC = {"h": True, "q": True, "k": True, "v": True, "z": True, "wo": False, "h2": True, "r": False,
        "dn": True, "up": False, "wt": False, "D": False}


def build(nc, x, ct, wmod, wat, wfa, wfb, cst, bcol, b2, ub, cb, out, scr, scw):
    plan = attention_plan() + ffn_plan()
    use, rd = {}, {}
    for ev in plan:
        if ev[0] in MISC:
            use[ev] = len(use)
            if MISC[ev[0]]:
                rd[ev] = len(rd)
    accs = [ev for ev in plan if ev[0] in ("acc",)]
    acc_no = {ev[1:]: n for n, ev in enumerate(accs)}
    last_chunk = {}
    first_chunk = {}
    for n in range(B * (NC + 1)):
        last_chunk[EXP_OF(n)] = n
        first_chunk.setdefault(EXP_OF(n), n)

    wo_before = {}
    for ev in plan:
        if ev[0] in ("h", "h2"):
            wo_before[ev] = sum(1 for w in plan[:plan.index(ev)] if w[0] == "wo")

    with ExitStack() as ctx:
        def sb(name, cols, dt=F32, parts=128):
            return ctx.enter_context(nc.sbuf_tensor(name, [parts, cols], dt))

        def sem(name):
            return ctx.enter_context(nc.semaphore(name))

        hh, hl = sb("hh", 4096, F32R), sb("hl", 4096, F32R)
        W = [sb("W0", 8192, F32R), sb("W1", 8192, F32R)]
        X = sb("X", 4096)
        tmp = sb("tmp", 1024)
        fb = sb("fb", 1024)
        stage = sb("stage", 2048)
        cc = sb("cc", C_END)
        gab = sb("gab", 2048)
        bc = sb("bc", B_END)
        rows = sb("rows", 128 + 1024, parts=8)
        oub = sb("oub", 256)
        modt = sb("modt", 32)
        sil = sb("sil", 24)
        mv = sb("mv", 8 + 24)
        rs = sb("rs", 16)
        sm = sb("sm", 4)
        nb = sb("nb", 4)
        ri = sb("ri", 4)
        wg = sb("wg", 128)
        rt = sb("rt", 256)
        ru = sb("ru", 32, U32)
        g0 = sb("g0", 20 + 160 + 8)
        Dm = sb("Dm", 128, parts=8)
        g0z = sb("g0z", 320, F32R)
        with ExitStack() as att:
            def sa(name, cols, dt=F32):
                return att.enter_context(nc.sbuf_tensor(name, [128, cols], dt))

            vh, vl = sa("vh", 2048, F32R), sa("vl", 2048, F32R)
            qk = sa("qk", 2048, F32R)
            zt = sa("zt", 4096, F32R)
            pth, ptl = sa("pth", 1280, F32R), sa("ptl", 1280, F32R)
            PB = sa("PB", 1280)
        Gr = sb("Gr", 4096, F32R)
        ur = sb("ur", 2048, F32R)
        gxh, gxl = sb("gxh", 2048, F32R), sb("gxl", 2048, F32R)
        oh, ol = sb("oh", 512, F32R), sb("ol", 512, F32R)
        G32 = sb("G32", 1024)
        prod = sb("prod", 1024)

        PS = [ctx.enter_context(nc.psum_tensor(f"S{n}", [128, 512], F32)) for n in range(3)]
        PT = [ctx.enter_context(nc.psum_tensor(f"T{n}", [128, 512], F32)) for n in range(2)] + [PS[2]]
        M = [ctx.enter_context(nc.psum_tensor(f"M{n}", [128, 512], F32)) for n in range(3)]

        ident = cc[:, C_ID:C_ID + 128]
        mask = cc[:, C_MASK:C_MASK + 512]

        s_x = [sem(f"s_x{b}") for b in range(B)]
        s_ct, s_wm, s_wm2, s_c, s_b, s_g = (sem(n) for n in ("s_ct", "s_wm", "s_wm2", "s_c", "s_b", "s_g"))
        s_st = [sem("s_st0"), sem("s_st1")]
        s_wh, s_wl, s_wd = sem("s_wh"), sem("s_wl"), sem("s_wd")
        s_sil, s_mod, s_mc, s_gr, s_gd = (sem(n) for n in ("s_sil", "s_mod", "s_mc", "s_gr", "s_gd"))
        mf, mh, me = sem("mf"), sem("mh"), sem("me")
        s_S, s_M, s_E, s_N, s_T = (sem(n) for n in ("s_S", "s_M", "s_E", "s_N", "s_T"))
        s_ph, s_pl = sem("s_ph"), sem("s_pl")
        s_v, s_a, s_mh = sem("s_v"), sem("s_a"), sem("s_mh")
        s_ve, s_r0, s_xn = sem("s_ve"), sem("s_r0"), sem("s_xn")
        s_lg, s_le, s_wg = sem("s_lg"), sem("s_le"), sem("s_wg")
        s_f1, s_gh, s_gl, s_o, s_ac = (sem(n) for n in ("s_f1", "s_gh", "s_gl", "s_o", "s_ac"))
        s_y, s_hs, s_xg, s_xl = (sem(n) for n in ("s_y", "s_hs", "s_xg", "s_xl"))
        s_g0, s_gz, s_dt, s_dc, s_dd, s_dm = (sem(n) for n in ("s_g0", "s_gz", "s_dt", "s_dc", "s_dd", "s_dm"))
        s_pa, s_oc = sem("s_pa"), sem("s_oc")
        s_ws = [sem(f"s_ws{t}") for t in range(B)]
        s_wb = [sem(f"s_wb{n}") for n in range(4)]
        s_fin, s_out = sem("s_fin"), sem("s_out")

        def bank(ev):
            return M[use[ev] % 3]

        def hT(b, k):
            s = slice(b * 1024 + k * 512, b * 1024 + k * 512 + 512)
            return hh[:, s], hl[:, s]

        def hTc(b, k, c):
            s = slice(b * 1024 + k * 512 + c * 128, b * 1024 + k * 512 + c * 128 + 128)
            return hh[:, s], hl[:, s]

        def wt(slot, at, n):
            return W[slot][:, at:at + n], W[slot][:, 4096 + at:4096 + at + n]

        def zs(h):
            return zt[:, h * 1024:h * 1024 + 512], zt[:, h * 1024 + 512:h * 1024 + 1024]

        def u_at(t):
            o = (t % 2) * 1024
            return ur[:, o:o + 512], ur[:, o + 512:o + 1024]

        def gx_at(t, k):
            o = (t % 2) * 1024 + k * 512
            return gxh[:, o:o + 512], gxl[:, o:o + 512]

        def u32(t):
            return stage[:, 512:1024] if t else fb[:, 512:1024]

        def acc_at(t):
            return stage[:, 1024 + (t % 2) * 512:1536 + (t % 2) * 512]

        def Gs(n):
            o = (n % 4) * 1024
            return Gr[:, o:o + 512], Gr[:, o + 512:o + 1024]

        def wb_at(i):
            o = (i % 2) * 512
            return (gab if i % 4 < 2 else tmp)[:, o:o + 512]

        def wT(t):
            return rows[0:8, 128 + (t % 2) * 512:640 + (t % 2) * 512]

        def lane(pair, a, n):
            return pair[0][:, a:a + n], pair[1][:, a:a + n]

        def piece(n):
            if n < 16:
                return wat[n // 4][:, (n % 4) * 1024:(n % 4) * 1024 + 1024], (n // 4) % 2, (n % 4) * 1024, 1024
            if n < 20:
                a = (n - 16) * 1024
                w = min(1024, F_END - a)
                return wfa[:, a:a + w], 0, a, w
            a = (n - 20) * 1024
            w = min(1024, W2_END - a)
            return wfb[:, a:a + w], 1, a, w

        def piece_after(n):
            if n < 8:
                return None
            if n < 20:
                return ("wo", 8 * (n // 4) - 9, 1)
            return ("v", NU // 2 - 1, 1)

        block = ctx.enter_context(nc.Block())

        @block.sync
        def _(sp):
            def load(n):
                src, _, _, w = piece(n)
                sp.dma_start(stage[:, (n % 2) * 1024:(n % 2) * 1024 + w], src).then_inc(s_st[n % 2], 16)

            def load_x(b):
                sp.dma_start(X[:, b * 1024:b * 1024 + 1024], x[:, b * 1024:b * 1024 + 1024]).then_inc(s_x[b], 16)

            load_x(0)
            sp.dma_start(cc[:], cst).then_inc(s_c, 16)
            load(0)
            load(1)
            load_x(1)
            for ev in plan:
                if ev[0] == "mod2":
                    sp.wait_ge(s_mod, 2)
                    load_x(2)
                    load_x(3)
                elif ev[0] == "wh":
                    n = ev[1]
                    if n + 2 < 23:
                        sp.wait_ge(s_wd, n + 1) if n < 2 else sp.wait_ge(s_wl, n - 1)
                        load(n + 2)
                elif ev[0] == "wt":
                    t = ev[1]
                    sp.wait_ge(me, use[ev] + 1)
                    sp.dma_start(scw[8 * t:8 * t + 8, :], wT(t)).then_inc(s_ws[t], 16)
                elif ev[0] == "wl":
                    i = ev[1]
                    sp.wait_ge(s_ws[i // 8], 16)
                    if i < 2:
                        sp.wait_ge(me, use[("wo", NU // 2 - 1, 1)] + 1)
                    elif i < 4:
                        sp.wait_ge(mf, use[("h2", 3, 1)] + 1)
                    else:
                        sp.wait_ge(s_ac, acc_no[divmod(i - 4, 8)[0], (i - 4) % 8 + 1] + 1)
                    sp.dma_start(wb_at(i), scw[i:i + 1, :].broadcast_to([128, 512])).then_inc(s_wb[i % 4], 16)
                elif ev[0] == "up" and ev[2] == 1:
                    t = ev[1]
                    sp.wait_ge(s_fin, 2 * t + 2)
                    sp.dma_start(out[:, t * 1024:t * 1024 + 1024],
                                 X[:, t * 1024:t * 1024 + 1024]).then_inc(s_out, 16)
            sp.wait_ge(s_out, 16 * B)

        @block.gpsimd
        def _(pool):
            pool.memset(rs[:, 12:16], -0.5).then_inc(s_mh, 1)
            pool.dma_start(bc[:], bcol).then_inc(s_b, 16)
            pool.dma_start(rows[:, 0:128], b2).then_inc(s_b, 16)
            pool.dma_start(oub[:], ub.broadcast_to([128, 256])).then_inc(s_b, 16)
            pool.dma_start(gab[:, 0:256], cb.broadcast_to([128, 256])).then_inc(s_b, 16)
            ln_no = 0
            pool_chain = 0
            for ev in plan:
                if ev[0] in ("lnp", "x2"):
                    if ln_no == 0:
                        pool.wait_ge(s_mh, 1)
                    pool.wait_ge(s_ve, ln_no + 1)
                    pool.tensor_tensor(rs[:, 4:8], rs[:, 0:4], rs[:, 12:16], ALU.pow).then_inc(s_r0, 1)
                    ln_no += 1
                if ev[0] == "mod2":
                    pool.wait_ge(s_gr, 1)
                    for n in range(2):
                        pool.dma_start(scr[n], rows[0:4, 640 + 256 * n:896 + 256 * n]).then_inc(s_gd, 16)
                    pool.wait_ge(s_gd, 32)
                    flat = scr.rearrange("(o a) b n -> o (a b n)", o=1)
                    pool.dma_start(gab[:], flat.broadcast_to([128, 2048])).then_inc(s_g, 16)
                if ev[0] == "acc" and ev[2] > 0:
                    _, t, e = ev
                    i = 8 * t + e - 1
                    pool.wait_ge(s_ac, acc_no[(t, e)] + 1)
                    pool.wait_ge(s_pa, i) if i else None
                    pool.tensor_tensor(acc_at(t), acc_at(t), prod[:, (i % 2) * 512:(i % 2) * 512 + 512],
                                       ALU.add).then_inc(s_pa, 1)
                if ev[0] == "wh" and ev[1] >= 2:
                    n = ev[1]
                    _, slot, a, w = piece(n)
                    hi, lo = wt(slot, a, w)
                    pool.wait_ge(s_wh, n + 1)
                    pool.tensor_tensor(lo, stage[:, (n % 2) * 1024:(n % 2) * 1024 + w], hi.bitcast(F32),
                                       ALU.subtract).then_inc(s_wl, 1)
                if ev[0] == "wo":
                    _, p, c2 = ev
                    a = unit(2 * p)[1] * 1024 + c2 * 512
                    pool.wait_ge(me, use[ev] + 1)
                    if p:
                        pool.wait_ge(s_y, 2 * p + c2 - 1)
                    pool.tensor_tensor(X[:, a:a + 512], X[:, a:a + 512], fb[:, c2 * 512:c2 * 512 + 512],
                                       ALU.add).then_inc(s_y, 1)
                if ev[0] == "gx":
                    t = ev[1]
                    pool.wait_ge(me, use[("h2", t, 1)] + 1)
                    pool.wait_ge(s_wl, 21)
                    for k in range(2):
                        a, l = hT(t, k)
                        pool.wait_ge(s_xg, 2 * t + k)
                        pool.tensor_tensor(stage[:, 0:512], a.bitcast(F32), l.bitcast(F32),
                                           ALU.add).then_inc(s_hs, 1)
                if ev[0] == "up":
                    _, t, c = ev
                    f = fb[:, c * 512:c * 512 + 512].rearrange("p (a n) -> p a n", a=2)
                    g = gab[:, 1024 + t * 256:1280 + t * 256].rearrange("p (a n) -> p a n", a=1)
                    y = X[:, t * 1024 + c * 512:t * 1024 + c * 512 + 512].rearrange("p (a n) -> p a n", a=2)
                    pool.wait_ge(me, use[ev] + 1)
                    pool.tensor_tensor(f, f, g.broadcast_to([128, 2, 256]), ALU.mult).then_inc(s_a, 1)
                    pool_chain += 1
                    pool.wait_ge(s_a, pool_chain)
                    pool.tensor_tensor(y, y, f, ALU.add).then_inc(s_fin, 1)

        @block.scalar
        def _(act):
            act.dma_start(sil[:, 0:8], ct).then_inc(s_ct, 16)
            act.dma_start(PB[:, 0:1024], wmod[:, 0:1024]).then_inc(s_wm, 16)
            act.dma_start(X[:, 2048:4096], wmod[:, 1024:3072]).then_inc(s_wm2, 16)
            r_no = 0
            for ev in plan:
                kind = ev[0]
                if kind == "mod":
                    act.wait_ge(s_ct, 16)
                    act.activation(sil[:, 8:16], sil[:, 0:8], ACT.Exp, scale=-1.0).then_inc(s_sil, 1)
                elif kind == "wh":
                    n = ev[1]
                    _, slot, a, w = piece(n)
                    act.wait_ge(s_st[n % 2], 16 * (n // 2 + 1))
                    if piece_after(n):
                        act.wait_ge(mf, use[piece_after(n)] + 1)
                    act.copy(wt(slot, a, w)[0], stage[:, (n % 2) * 1024:(n % 2) * 1024 + w]).then_inc(s_wh, 1)
                elif kind in ("h", "h2"):
                    _, b, k = ev
                    o = 0 if kind == "h" else 16
                    act.wait_ge(mf, use[ev] + 1)
                    if use[ev] == 0:
                        act.wait_ge(s_mc, 1)
                    act.activation(hT(b, k)[0], bank(ev)[:], ACT.Identity,
                                   bias=modt[:, o + 4 * k + b:o + 4 * k + b + 1],
                                   scale=modt[:, o + 8 + 4 * k + b:o + 9 + 4 * k + b]).then_inc(mh, 1)
                elif kind in ("q", "k", "v", "z"):
                    act.wait_ge(mf, use[ev] + 1)
                    if kind == "q":
                        dst = qk[:, 0:512]
                    elif kind == "k":
                        dst = qk[:, 1024:1536]
                    elif kind == "v":
                        o = (ev[1] % 2) * 1024 + ev[2] * 512
                        dst = vh[:, o:o + 512]
                    else:
                        dst = zs(ev[1] % 4)[0]
                    act.copy(dst, bank(ev)[:]).then_inc(mh, 1)
                elif kind == "S":
                    u = ev[1]
                    for n, (bk, chunks) in enumerate(S_ORDER):
                        act.wait_ge(s_M, 3 * u + n + 1)
                        if u > 0 and n == 0:
                            act.wait_ge(s_N, u)
                        for i in chunks:
                            w = 128 * (i + 1)
                            a = S_AT[i][1]
                            ins = act.activation(PB[:, P_OFF[i]:P_OFF[i] + w], PS[bk][:, a:a + w], ACT.Exp,
                                                 bias=nb[:, i:i + 1], scale=-1.0, accum_out=sm[:, i:i + 1])
                        ins.then_inc(s_E, 1)
                elif kind == "T":
                    u = ev[1]
                    for n, (bk, _) in enumerate(T_ORDER):
                        a, z = T_COLS[bk]
                        act.wait_ge(s_T, 3 * u + n + 1)
                        act.copy(pth[:, a:z], PT[bk][:, 0:z - a]).then_inc(s_ph, 1)
                elif kind == "r":
                    act.wait_ge(s_lg, 2 * r_no + 1)
                    act.activation(rt[:, 64:96], rt[:, 32:64], ACT.Exp).then_inc(s_le, 1)
                    act.wait_ge(s_lg, 2 * r_no + 2)
                    act.activation(rt[:, 168:172], rt[:, 160:164], ACT.Exp).then_inc(s_le, 1)
                    r_no += 1
                elif kind == "d0":
                    act.wait_ge(s_b, 64)
                    act.activation(g0[:, 0:20], bc[:, B_B1:B_B1 + 20], ACT.Gelu).then_inc(s_g0, 1)
                elif kind == "dn":
                    t = ev[1]
                    act.wait_ge(mf, use[ev] + 1)
                    if t == 0:
                        act.wait_ge(s_b, 64)
                    if t == 0:
                        act.wait_ge(s_y, NU)
                    else:
                        act.wait_ge(s_xl, 2 * t)
                    act.activation(u32(t), bank(ev)[:], ACT.Gelu,
                                   bias=bc[:, B_DOWN:B_DOWN + 1]).then_inc(s_v, 1)
                    act.activation(u_at(t)[0], bank(ev)[:], ACT.Gelu,
                                   bias=bc[:, B_DOWN:B_DOWN + 1]).then_inc(mh, 1)
                elif kind == "gx":
                    t = ev[1]
                    act.wait_ge(me, use[("dn", t)] + 1)
                    if t >= 2:
                        act.wait_ge(mf, use[("up", t - 2, 1)] + 1)
                    for k in range(2):
                        act.wait_ge(s_hs, 2 * t + k + 1)
                        if k:
                            act.wait_ge(s_xl, 2 * t + 1)
                        act.activation(stage[:, 512:1024], stage[:, 0:512], ACT.Gelu).then_inc(s_v, 1)
                        act.activation(gx_at(t, k)[0], stage[:, 0:512], ACT.Gelu).then_inc(s_xg, 1)
                elif kind == "w1":
                    n = ev[1]
                    t, j = divmod(n, NC + 1)
                    bias = bc[:, B_SH1:B_SH1 + 1] if j == 0 else bc[:, B_B1 + j - 1:B_B1 + j]
                    act.wait_ge(s_f1, n + 1)
                    act.wait_ge(s_gl, n - 1) if n >= 2 else None
                    act.activation(G32[:, (n % 2) * 512:(n % 2) * 512 + 512], PS[n % 3][:], ACT.Gelu,
                                   bias=bias).then_inc(s_v, 1)
                    act.activation(Gs(n)[0], PS[n % 3][:], ACT.Gelu, bias=bias).then_inc(s_gh, 1)

        @block.tensor
        def _(pe):
            def mm3(o, lhs, rhs, start, stop, **kw):
                pe.matmul(o, lhs[0], rhs[0], start=start, stop=False, **kw)
                pe.matmul(o, lhs[0], rhs[1], start=False, stop=False, **kw)
                return pe.matmul(o, lhs[1], rhs[0], start=False, stop=stop, **kw)

            ln_no = 0
            for ev in plan:
                kind = ev[0]
                if kind in MISC:
                    m = use[ev]
                    o = bank(ev)
                    if m >= 3:
                        pe.wait_ge(me, m - 2)
                if kind == "mod":
                    pe.wait_ge(s_wm, 16)
                    pe.wait_ge(s_sil, 2)
                    wm = PB[:, 0:1024].rearrange("p (k n) -> p k n", k=2)
                    sl = sil[:, 16:24].rearrange("p (k n) -> p k n", k=2)
                    for n in range(4):
                        for k in range(2):
                            ins = pe.matmul(PS[0][:, 4 * n:4 * n + 4], wm[:, k, 128 * n:128 * n + 128], sl[:, k, :],
                                            start=(k == 0), stop=(k == 1))
                    ins.then_inc(s_mod, 1)
                elif kind == "mod2":
                    pe.wait_ge(s_wm2, 16)
                    pe.wait_ge(s_mc, 1)
                    wm = X[:, 2048:4096].rearrange("p (k n) -> p k n", k=2)
                    for k in range(2):
                        pe.matmul(PS[1][0:4, :], sl[:, k, :], wm[:, k, 0:512], start=(k == 0), stop=(k == 1))
                    for n in range(4):
                        for k in range(2):
                            ins = pe.matmul(PS[0][:, 4 * n:4 * n + 4], wm[:, k, 512 + 128 * n:640 + 128 * n],
                                            sl[:, k, :], start=(k == 0), stop=(k == 1))
                    ins.then_inc(s_mod, 1)
                elif kind in ("h", "h2"):
                    _, b, k = ev
                    if k == 0:
                        pe.wait_ge(s_xn, ln_no + 1)
                        ln_no += 1
                    if m == 0:
                        pe.wait_ge(s_c, 16)
                    for c in range(4):
                        ins = pe.transpose(o[:, 128 * c:128 * c + 128],
                                           tmp[:, 256 * c + 128 * k:256 * c + 128 * k + 128], ident)
                    ins.then_inc(mf, 1)
                elif kind in ("q", "k"):
                    g, b, h = unit(ev[1])
                    if h == 0:
                        pe.wait_ge(me, use[("h", b, 1)] + 1)
                        pc = 4 * g + (kind == "k")
                        pe.wait_ge(s_wd, pc + 1) if g == 0 else pe.wait_ge(s_wl, pc - 1)
                    a = (kind == "k") * 1024 + h * 128
                    for k in range(2):
                        ins = mm3(o[:], wt(g % 2, a + 512 * k, 128), hT(b, k), k == 0, k == 1)
                    ins.then_inc(mf, 1)
                elif kind == "v":
                    _, p, c2 = ev
                    g, b, h = unit(2 * p)
                    pe.wait_ge(s_wl, 4 * g + 1)
                    for c in range(2):
                        for k in range(2):
                            ins = mm3(o[:, 256 * c:256 * c + 256], hTc(b, k, 2 * c2 + c),
                                      wt(g % 2, 2048 + 512 * k + 128 * h, 256), k == 0, k == 1)
                    ins.then_inc(mf, 1)
                elif kind == "S":
                    u = ev[1]
                    pe.wait_ge(me, use[("k", u)] + 1)
                    if u == 0:
                        pe.wait_ge(s_gr, 1)
                    q = (qk[:, 0:512], qk[:, 512:1024])
                    kk = (qk[:, 1024:1536], qk[:, 1536:2048])
                    for n, (bk, chunks) in enumerate(S_ORDER):
                        if u > 0:
                            pe.wait_ge(s_E, 3 * u - 3 + n + 1)
                            if bk == 2:
                                pe.wait_ge(s_pl, 3 * u - 2)
                        for i in chunks:
                            a, w = S_AT[i][1], 128 * (i + 1)
                            ins = mm3(PS[bk][:, a:a + w], lane(q, 128 * i, 128), lane(kk, 0, w), True, True)
                        ins.then_inc(s_S, 1)
                elif kind == "T":
                    u = ev[1]
                    pe.wait_ge(s_N, u + 1)
                    for n, (bk, chunks) in enumerate(T_ORDER):
                        if u > 0:
                            pe.wait_ge(s_pl, 3 * u - 3 + n + 1)
                        for j in chunks:
                            a = T_AT[j]
                            for i in range(j, 4):
                                ins = pe.transpose(PT[bk][:, a + 128 * (i - j):a + 128 * (i - j) + 128],
                                                   PB[:, P_OFF[i] + 128 * j:P_OFF[i] + 128 * j + 128], ident)
                        ins.then_inc(s_T, 1)
                elif kind == "z":
                    u = ev[1]
                    h = u % 4
                    pe.wait_ge(me, use[("v", u // 2, 1)] + 1)
                    va = (u // 2 % 2) * 1024 + (u % 2) * 128
                    pe.wait_ge(s_pl, 3 * u + 3)
                    for j in range(4):
                        w = 512 - 128 * j
                        ins = mm3(o[:, 128 * j:512], (vh[:, va + 256 * j:va + 256 * j + 128],
                                                      vl[:, va + 256 * j:va + 256 * j + 128]),
                                  (pth[:, T_OFF[j]:T_OFF[j] + w], ptl[:, T_OFF[j]:T_OFF[j] + w]), j == 0, j == 3)
                    ins.then_inc(mf, 1)
                elif kind == "wo":
                    _, p, c2 = ev
                    g = unit(2 * p)[0]
                    pe.wait_ge(me, use[("z", 2 * p + 1)] + 1)
                    pe.wait_ge(s_wl, 4 * g + 2)
                    for c in range(2):
                        for n in range(2):
                            h = (2 * p + n) % 4
                            ins = mm3(o[:, 256 * c:256 * c + 256], lane(zs(h), 256 * c2 + 128 * c, 128),
                                      wt(g % 2, 3072 + 256 * h, 256), n == 0, n == 1)
                    ins.then_inc(mf, 1)
                elif kind == "r":
                    b = ev[1]
                    pe.wait_ge(s_wl, 18)
                    pe.wait_ge(me, use[("h2", b, 1)] + 1)
                    for c in range(4):
                        for k in range(2):
                            l, r = hTc(b, k, c), wt(0, F_RT + 8 * k, 8)
                            ins = mm3(o[:, 8 * c:8 * c + 8], l, r, k == 0, k == 1)
                    ins.then_inc(mf, 1)
                elif kind == "dn":
                    t = ev[1]
                    pe.wait_ge(s_wl, 18)
                    pe.wait_ge(me, use[("h2", t, 1)] + 1)
                    for k in range(2):
                        ins = mm3(o[:], wt(0, F_DOWN + 128 * k, 128), hT(t, k), k == 0, k == 1)
                    ins.then_inc(mf, 1)
                elif kind == "w1":
                    n = ev[1]
                    t, j = divmod(n, NC + 1)
                    if j == 0:
                        pe.wait_ge(me, use[("dn", t)] + 1)
                    if n >= 3:
                        pe.wait_ge(s_gh, n - 2)
                    else:
                        pe.wait_ge(s_E, 3 * NU)
                    a = F_SH1 if j == 0 else F_W1 + 128 * (j - 1)
                    mm3(PS[n % 3][:], wt(0, a, 128), u_at(t), True, True).then_inc(s_f1, 1)
                elif kind == "w2":
                    n = ev[1]
                    t, j = divmod(n, NC + 1)
                    X_ = acc_no[EXP_OF(n)]
                    first, last = first_chunk[EXP_OF(n)] == n, last_chunk[EXP_OF(n)] == n
                    pe.wait_ge(s_gl, n + 1)
                    if n == 0:
                        pe.wait_ge(s_pl, 3 * NU)
                    if n == 1:
                        pe.wait_ge(s_wl, 21)
                    if first and X_ >= 2:
                        pe.wait_ge(s_ac, X_ - 1)
                    w = wt(0, F_SH2, 128) if j == 0 else wt(1, 128 * (j - 1), 128)
                    ins = mm3(PT[X_ % 2][:], w, Gs(n), first, last)
                    if last:
                        ins.then_inc(s_o, 1)
                elif kind == "dt":
                    pe.wait_ge(s_wl, 21)
                    pe.wait_ge(s_gz, 1)
                    o = M[use[("D", 0)] % 3]
                    pe.wait_ge(me, use[("D", 0)] - 2)
                    for c in range(NC):
                        w = wt(1, 128 * c, 128)
                        ins = mm3(o[:, 0:8], w, (g0z[:, 8 * c:8 * c + 8], g0z[:, 160 + 8 * c:168 + 8 * c]),
                                  c == 0, c == NC - 1)
                    ins.then_inc(s_dt, 1)
                    pe.wait_ge(s_dc, 1)
                    pe.matmul(o[0:8, 128:256], g0[:, 180:188], ident, start=True, stop=False)
                    pe.matmul(o[0:8, 128:256], cc[0:8, C_ONE:C_ONE + 8], rows[0:8, 0:128],
                              start=False, stop=True).then_inc(s_dd, 1)
                elif kind == "wt":
                    t = ev[1]
                    pe.wait_ge(s_wg, t + 1)
                    for c in range(4):
                        ins = pe.matmul(o[0:8, 128 * c:128 * c + 128], wg[:, 32 * t + 8 * c:32 * t + 8 * c + 8],
                                        ident, start=True, stop=True)
                    ins.then_inc(mf, 1)
                elif kind == "D":
                    t = ev[1]
                    pe.wait_ge(me, use[("wt", t)] + 1)
                    if t == 0:
                        pe.wait_ge(s_dm, 1)
                    pe.matmul(o[:], Dm[0:8, :], wT(t), start=True, stop=True).then_inc(mf, 1)
                elif kind == "up":
                    _, t, c2 = ev
                    pe.wait_ge(s_oc, t + 1)
                    pe.wait_ge(s_xl, 2 * t + 2)
                    for c in range(2):
                        cx = 2 * c2 + c
                        oo = o[:, 256 * c:256 * c + 256]
                        mm3(oo, lane((oh, ol), 128 * cx, 128),
                            wt(0, F_UP, 256), True, False)
                        for k in range(2):
                            ins = mm3(oo, lane(gx_at(t, k), 128 * cx, 128), wt(0, F_CORE + 256 * k, 256),
                                      False, k == 1)
                    ins.then_inc(mf, 1)

        @block.vector
        def _(v):
            chain = [0]
            s_l = ctx.enter_context(nc.semaphore("s_l"))

            def link(ins):
                chain[0] += 1
                ins.then_inc(s_l, 1)
                v.wait_ge(s_l, chain[0])

            def bcast(ap, shape):
                return ap.broadcast_to(shape)

            def normal(n, src, parts=4):
                for c in range(parts):
                    ins = v.bn_stats(mv[:, 8 + 6 * c:14 + 6 * c], src[:, 256 * c:256 * c + 256])
                link(ins)
                for c in range(parts):
                    ins = v.bn_aggr(mv[:, 2 * c:2 * c + 2], mv[:, 8 + 6 * c:14 + 6 * c])
                link(ins)
                v.tensor_scalar(rs[:, 0:4], mv[:, 1:8:2], 1e-5, None, ALU.add).then_inc(s_ve, 1)
                v.wait_ge(s_r0, n + 1)
                for c in range(parts):
                    ins = v.tensor_scalar(tmp[:, 256 * c:256 * c + 256], src[:, 256 * c:256 * c + 256],
                                          mv[:, 2 * c:2 * c + 1], rs[:, 4 + c:5 + c], ALU.subtract, ALU.mult)
                ins.then_inc(s_xn, 1)

            ln_no = 0
            r_no = 0
            fb_held = [0, 0]
            xv = 0
            for ev in plan:
                kind = ev[0]
                if kind == "mod":
                    v.wait_ge(s_sil, 1)
                    link(v.tensor_scalar(sil[:, 16:24], sil[:, 8:16], 1.0, None, ALU.add))
                    link(v.reciprocal(sil[:, 16:24], sil[:, 16:24]))
                    v.tensor_tensor(sil[:, 16:24], sil[:, 16:24], sil[:, 0:8], ALU.mult).then_inc(s_sil, 1)
                    v.wait_ge(s_mod, 1)
                    v.tensor_copy(modt[:, 0:8], PS[0][:, 0:8])
                    v.tensor_scalar(modt[:, 8:16], PS[0][:, 8:16], 1.0, None, ALU.add).then_inc(s_mc, 1)
                elif kind == "mod2":
                    v.wait_ge(s_b, 64)
                    v.tensor_tensor(oub[:], oub[:], gab[:, 0:256], ALU.add)
                    v.tensor_scalar(bc[:, B_SH2:B_SH2 + 1], bc[:, B_SH2:B_SH2 + 1], 0.1, None, ALU.mult)
                    v.wait_ge(s_mod, 2)
                    v.tensor_copy(modt[:, 16:24], PS[0][:, 0:8])
                    v.tensor_scalar(modt[:, 24:32], PS[0][:, 8:16], 1.0, None, ALU.add)
                    rg = rows[0:4, 640:1152]
                    link(v.tensor_scalar(rg, PS[1][0:4, :], -1.0, 0.25, ALU.mult, ALU.max))
                    link(v.tensor_tensor(rg, PS[1][0:4, :], rg, ALU.max))
                    sg = PB[0:4, 0:512]
                    link(v.tensor_scalar(sg, PS[1][0:4, :], 0.0, 2.0, ALU.is_ge, ALU.mult))
                    v.scalar_tensor_tensor(out=rg, in0=sg, scalar=-1.0, in1=rg, op0=ALU.add,
                                           op1=ALU.mult).then_inc(s_gr, 1)
                elif kind == "wh" and ev[1] < 2:
                    n = ev[1]
                    _, slot, a, w = piece(n)
                    hi, lo = wt(slot, a, w)
                    v.wait_ge(s_wh, n + 1)
                    v.tensor_tensor(lo, stage[:, n * 1024:n * 1024 + w], hi.bitcast(F32), ALU.subtract)\
                     .then_inc(s_wd, 1)
                elif kind == "lnp":
                    b = ev[1]
                    v.wait_ge(s_x[b], 16)
                    if b:
                        v.wait_ge(mf, use[("h", b - 1, 1)] + 1)
                    normal(ln_no, X[:, b * 1024:b * 1024 + 1024])
                    ln_no += 1
                elif kind in ("h", "h2"):
                    _, b, k = ev
                    o = 0 if kind == "h" else 16
                    hi, lo = hT(b, k)
                    v.wait_ge(mh, rd[ev] + 1)
                    fbuf = fb[:, 512 * k:512 * k + 512]
                    v.wait_ge(s_y, wo_before[ev])
                    if fb_held[k]:
                        v.wait_ge(me, fb_held[k])
                    fb_held[k] = use[ev] + 1
                    link(v.tensor_scalar(fbuf, bank(ev)[:], modt[:, o + 8 + 4 * k + b:o + 9 + 4 * k + b],
                                         modt[:, o + 4 * k + b:o + 4 * k + b + 1], ALU.mult, ALU.add))
                    v.tensor_tensor(lo, fbuf, hi.bitcast(F32), ALU.subtract).then_inc(me, 1)
                elif kind in ("q", "k", "v", "z"):
                    v.wait_ge(mh, rd[ev] + 1)
                    if kind == "q":
                        hi, lo = qk[:, 0:512], qk[:, 512:1024]
                    elif kind == "k":
                        hi, lo = qk[:, 1024:1536], qk[:, 1536:2048]
                    elif kind == "v":
                        o = (ev[1] % 2) * 1024 + ev[2] * 512
                        s = slice(o, o + 512)
                        hi, lo = vh[:, s], vl[:, s]
                    else:
                        hi, lo = zs(ev[1] % 4)
                    v.tensor_tensor(lo, bank(ev)[:], hi.bitcast(F32), ALU.subtract).then_inc(me, 1)
                elif kind == "S":
                    u = ev[1]
                    if u > 0:
                        v.wait_ge(s_E, 3 * u)
                    for n, (bk, chunks) in enumerate(S_ORDER):
                        v.wait_ge(s_S, 3 * u + n + 1)
                        for i in chunks:
                            a, w = S_AT[i][1], 128 * (i + 1)
                            ins = v.tensor_tensor_reduce(PS[bk][:, a:a + w], PS[bk][:, a:a + w],
                                                         mask[:, 512 - w:512], -INV, BIG, ALU.add, ALU.min,
                                                         nb[:, i:i + 1])
                        ins.then_inc(s_M, 1)
                elif kind == "norm":
                    u = ev[1]
                    v.wait_ge(s_E, 3 * u + 3)
                    link(v.reciprocal(ri[:], sm[:]))
                    for i in (1, 0, 2, 3):
                        p = PB[:, P_OFF[i]:P_OFF[i] + 128 * (i + 1)]
                        ins = v.tensor_scalar(p, p, ri[:, i:i + 1], None, ALU.mult)
                    ins.then_inc(s_N, 1)
                elif kind == "T":
                    u = ev[1]
                    for n, (bk, _) in enumerate(T_ORDER):
                        a, z = T_COLS[bk]
                        v.wait_ge(s_ph, 3 * u + n + 1)
                        v.tensor_tensor(ptl[:, a:z], PT[bk][:, 0:z - a], pth[:, a:z].bitcast(F32),
                                        ALU.subtract).then_inc(s_pl, 1)
                elif kind == "wo":
                    _, p, c2 = ev
                    b = unit(2 * p)[1]
                    v.wait_ge(mf, use[ev] + 1)
                    if p:
                        v.wait_ge(s_y, 2 * p + c2 - 1)
                    if fb_held[c2]:
                        v.wait_ge(me, fb_held[c2])
                        fb_held[c2] = 0
                    if p == 0:
                        v.wait_ge(s_g, 16)
                    ga = gab[:, b * 256:b * 256 + 256].rearrange("p (a n) -> p a n", a=1)
                    v.tensor_tensor(fb[:, c2 * 512:c2 * 512 + 512].rearrange("p (a n) -> p a n", a=2),
                                    bank(ev)[:].rearrange("p (a n) -> p a n", a=2), bcast(ga, [128, 2, 256]),
                                    ALU.mult).then_inc(me, 1)
                elif kind == "x2":
                    b = ev[1]
                    v.wait_ge(s_y, 2 * (25 + 2 * b) + 2)
                    v.wait_ge(mf, use[("h2", b - 1, 1) if b else ("h", 3, 1)] + 1)
                    normal(ln_no, X[:, b * 1024:b * 1024 + 1024])
                    ln_no += 1
                elif kind == "r":
                    b = ev[1]
                    v.wait_ge(mf, use[ev] + 1)
                    L = rt[:, 0:32]
                    L3 = L.rearrange("p (a n) -> p a n", a=4)
                    rb = cc[:, C_RB:C_RB + 8].rearrange("p (a n) -> p a n", a=1)
                    co = cc[:, C_COST:C_COST + 8].rearrange("p (a n) -> p a n", a=1)
                    io = cc[:, C_IOTA:C_IOTA + 8].rearrange("p (a n) -> p a n", a=1)
                    v.tensor_tensor(L3, bank(ev)[:, 0:32].rearrange("p (a n) -> p a n", a=4),
                                    bcast(rb, [128, 4, 8]), ALU.add).then_inc(me, 1)
                    v.wait_ge(me, use[ev] + 1)
                    link(v.tensor_tensor(L3, L3, bcast(co, [128, 4, 8]), ALU.subtract))
                    mx = rt[:, 96:100]

                    def per(ap):
                        return bcast(ap.rearrange("p (a n) -> p a n", n=1), [128, 4, 8])

                    link(v.tensor_reduce(mx, L3, AX.X, ALU.max))
                    e0 = rt[:, 32:64]
                    v.tensor_tensor(e0.rearrange("p (a n) -> p a n", a=4), L3, per(mx), ALU.subtract)\
                     .then_inc(s_lg, 1)
                    v.wait_ge(s_le, 2 * r_no + 1)
                    pr = rt[:, 64:96]
                    pr3 = pr.rearrange("p (a n) -> p a n", a=4)
                    link(v.tensor_reduce(mx, pr3, AX.X, ALU.add))
                    link(v.reciprocal(mx, mx))
                    link(v.tensor_tensor(pr3, pr3, per(mx), ALU.mult))
                    for c in range(4):
                        ins = v.max(rt[:, 128 + 8 * c:136 + 8 * c], pr[:, 8 * c:8 * c + 8])
                    link(ins)
                    for c in range(4):
                        ins = v.max_index(ru[:, 8 * c:8 * c + 8], rt[:, 128 + 8 * c:136 + 8 * c],
                                          pr[:, 8 * c:8 * c + 8])
                    link(ins)
                    idx = rt[:, 0:32]
                    link(v.tensor_copy(idx, ru[:]))
                    v.tensor_tensor(rt[:, 160:164], rt[:, 129:160:8], rt[:, 128:160:8], ALU.subtract)\
                     .then_inc(s_lg, 1)
                    v.wait_ge(s_le, 2 * r_no + 2)
                    ee, ga_, gb_ = rt[:, 168:172], rt[:, 172:176], rt[:, 176:180]
                    link(v.tensor_scalar(ga_, ee, 1.0, None, ALU.add))
                    link(v.reciprocal(ga_, ga_))
                    link(v.tensor_tensor(gb_, ga_, ee, ALU.mult))
                    a3 = rt[:, 32:64].rearrange("p (a n) -> p a n", a=4)
                    b3 = rt[:, 64:96].rearrange("p (a n) -> p a n", a=4)
                    io4 = bcast(io, [128, 4, 8])
                    v.tensor_tensor(a3, io4, per(idx[:, 0:32:8]), ALU.is_equal)
                    link(v.tensor_tensor(b3, io4, per(idx[:, 1:32:8]), ALU.is_equal))
                    v.tensor_tensor(a3, a3, per(ga_), ALU.mult)
                    link(v.tensor_tensor(b3, b3, per(gb_), ALU.mult))
                    v.tensor_tensor(wg[:, 32 * b:32 * b + 32].rearrange("p (a n) -> p a n", a=4), a3, b3, ALU.add)\
                     .then_inc(s_wg, 1)
                    v.wait_ge(s_wg, r_no + 1)
                    r_no += 1
                elif kind == "d0":
                    v.wait_ge(s_g0, 1)
                    gz = g0[:, 20:180]
                    a = g0[:, 0:20].rearrange("p (a n) -> p a n", n=1)
                    ex = cc[:, C_EXM:C_EXM + 160].rearrange("p (a n) -> p a n", n=8)
                    link(v.tensor_tensor(gz.rearrange("p (a n) -> p a n", n=8), ex, bcast(a, [128, 20, 8]), ALU.mult))
                    link(v.tensor_copy(g0z[:, 0:160], gz))
                    v.tensor_tensor(g0z[:, 160:320], gz, g0z[:, 0:160].bitcast(F32), ALU.subtract).then_inc(s_gz, 1)
                elif kind == "dt":
                    o = M[use[("D", 0)] % 3]
                    v.wait_ge(s_dt, 1)
                    v.tensor_copy(g0[:, 180:188], o[:, 0:8]).then_inc(s_dc, 1)
                    v.wait_ge(s_dd, 1)
                    v.tensor_copy(Dm[0:8, :], o[0:8, 128:256]).then_inc(s_dm, 1)
                elif kind == "wt":
                    v.wait_ge(mf, use[ev] + 1)
                    if ev[1] == 0:
                        v.wait_ge(s_gd, 32)
                    elif ev[1] >= 2:
                        v.wait_ge(s_ws[ev[1] - 2], 16)
                        v.wait_ge(mf, use[("D", ev[1] - 2)] + 1)
                    v.tensor_copy(wT(ev[1]), bank(ev)[0:8, :]).then_inc(me, 1)
                elif kind == "D":
                    t = ev[1]
                    v.wait_ge(mf, use[ev] + 1)
                    if t == 0:
                        v.wait_ge(s_wl, 21)
                    v.tensor_scalar(acc_at(t), bank(ev)[:], bc[:, B_SH2:B_SH2 + 1], None, ALU.add).then_inc(me, 1)
                elif kind == "acc":
                    _, t, e = ev
                    n = acc_no[(t, e)]
                    v.wait_ge(s_o, n + 1)
                    if e == 0:
                        v.wait_ge(me, use[("D", t)] + 1)
                        v.scalar_tensor_tensor(out=acc_at(t), in0=PT[n % 2][:], scalar=0.1, in1=acc_at(t),
                                               op0=ALU.mult, op1=ALU.add).then_inc(s_ac, 1)
                    else:
                        i = 8 * t + e - 1
                        v.wait_ge(s_wb[i % 4], 16 * (i // 4 + 1))
                        if i >= 2:
                            v.wait_ge(s_pa, i - 1)
                        v.tensor_tensor(prod[:, (i % 2) * 512:(i % 2) * 512 + 512], PT[n % 2][:], wb_at(i),
                                        ALU.mult).then_inc(s_ac, 1)
                elif kind == "o":
                    t = ev[1]
                    v.wait_ge(s_pa, 8 * t + 8)
                    if t:
                        v.wait_ge(mf, use[("up", t - 1, 1)] + 1)
                    link(v.tensor_copy(oh[:], acc_at(t)))
                    v.tensor_tensor(ol[:], acc_at(t), oh[:].bitcast(F32), ALU.subtract).then_inc(s_oc, 1)
                elif kind == "dn":
                    v.wait_ge(mh, rd[ev] + 1)
                    xv += 1
                    v.wait_ge(s_v, xv)
                    hi, lo = u_at(ev[1])
                    v.tensor_tensor(lo, u32(ev[1]), hi.bitcast(F32), ALU.subtract).then_inc(me, 1)
                elif kind == "gx":
                    t = ev[1]
                    for k in range(2):
                        xv += 1
                        v.wait_ge(s_xg, 2 * t + k + 1)
                        v.wait_ge(s_v, xv)
                        hi, lo = gx_at(t, k)
                        v.tensor_tensor(lo, stage[:, 512:1024], hi.bitcast(F32), ALU.subtract).then_inc(s_xl, 1)
                elif kind == "w1":
                    n = ev[1]
                    xv += 1
                    v.wait_ge(s_gh, n + 1)
                    v.wait_ge(s_v, xv)
                    hi, lo = Gs(n)
                    v.tensor_tensor(lo, G32[:, (n % 2) * 512:(n % 2) * 512 + 512], hi.bitcast(F32),
                                    ALU.subtract).then_inc(s_gl, 1)
                elif kind == "up":
                    _, t, c2 = ev
                    v.wait_ge(mf, use[ev] + 1)
                    if t:
                        v.wait_ge(s_fin, 2 * t - 1 + c2)
                    f = fb[:, 512 * c2:512 * c2 + 512].rearrange("p (a n) -> p a n", a=2)
                    ob = oub[:].rearrange("p (a n) -> p a n", a=1)
                    v.tensor_tensor(f, bank(ev)[:].rearrange("p (a n) -> p a n", a=2), bcast(ob, [128, 2, 256]),
                                    ALU.add).then_inc(me, 1)


def kernel(**inputs):
    import numpy as np
    import concourse.bacc as bacc
    from concourse.bass_utils import run_bass_kernel_spmd

    A = {k: np.asarray(v) for k, v in inputs.items()}
    f = "L0_ffn_"

    def rowsplit(w):
        k = w.shape[0] // 128
        return w.reshape(k, 128, -1).transpose(1, 0, 2).reshape(128, -1)

    def perhead(w):
        return w.reshape(4, 4, 128, 2, 128).transpose(0, 4, 3, 1, 2).reshape(4, 128, 1024)

    wo = A["L0_attn_W_O"].reshape(256, 4, 4, 128).transpose(1, 3, 2, 0).reshape(4, 128, 1024)
    wat = np.concatenate([perhead(A["L0_attn_W_Q"]), perhead(A["L0_attn_W_K"]), perhead(A["L0_attn_W_V"]), wo], 2)
    wfa = np.concatenate([A[f"{f}e{e}_w1"] for e in range(8)] +
                         [rowsplit(A[f + "down_w"]), rowsplit(A[f + "core_w"]), A[f + "shared_w1"],
                          A[f + "shared_w2"], A[f + "up_w"], rowsplit(A[f + "router_w"])], 1)
    wfb = np.concatenate([rowsplit(A[f"{f}e{e}_w2"]) for e in range(8)], 1)
    b1 = np.concatenate([A[f"{f}e{e}_b1"].reshape(-1, 128).T for e in range(8)], 1)
    bcol = np.concatenate([A[f + "down_b"][:, None], A[f + "shared_b1"][:, None], b1,
                           A[f + "shared_b2"][:, None]], 1)
    b2 = np.stack([A[f"{f}e{e}_b2"] for e in range(8)])
    cst = np.zeros((128, C_END), np.float32)
    cst[:, C_ID:C_ID + 128] = np.eye(128)
    cst[:, C_MASK + 384:C_MASK + 512] = np.where(np.tril(np.ones((128, 128))) > 0, 0, -1e10)
    for c, e in enumerate(EXPERT):
        cst[:, C_EXM + 8 * c:C_EXM + 8 * c + 8] = np.arange(8) != e
    cst[:, C_IOTA:C_IOTA + 8] = np.arange(8)
    cst[:, C_COST:C_COST + 8] = np.float32(1e-7) * (np.array(HID, np.float32) * 256)
    cst[:, C_ONE:C_ONE + 8] = 1
    cst[:, C_RB:C_RB + 8] = A[f + "router_b"][None]
    wm = A["L0_wmod"]
    wm = np.concatenate([wm[:, 0:768], wm[:, 1280:1536], wm[:, 768:1280]], 1)
    ins = {
        "x": rowsplit(A["L0_attn_x"].reshape(2048, 256)),
        "ct": rowsplit(np.ascontiguousarray(A["L0_c"].T)),
        "wmod": np.concatenate([rowsplit(wm[:, 0:512]), rowsplit(wm[:, 512:])], 1),
        "wat": wat, "wfa": wfa, "wfb": wfb, "cst": cst, "bcol": bcol, "b2": b2,
        "ub": A[f + "up_b"][None], "cb": A[f + "core_b"][None], 
    }
    nc = bacc.Bacc("TRN2", target_bir_lowering=False, num_devices=1)
    arrays, aps = {}, {}
    for name, a in ins.items():
        arrays["in_" + name] = np.ascontiguousarray(a)
        aps[name] = nc.dram_tensor("in_" + name, a.shape, F32, kind="ExternalInput").ap()
    out = nc.dram_tensor("out_0", (128, 4096), F32, kind="ExternalOutput").ap()
    scr = nc.dram_tensor("scr", (2, 4, 256), F32, kind="Internal").ap()
    scw = nc.dram_tensor("scw", (8 * B, 512), F32, kind="Internal").ap()
    build(nc, **aps, out=out, scr=scr, scw=scw)
    r = run_bass_kernel_spmd(nc, [arrays], core_ids=[0])
    y = np.asarray(r.results[0]["out_0"])
    return y.reshape(128, 16, 256).transpose(1, 0, 2).reshape(4, 512, 256)
```

```python
from contextlib import ExitStack

import concourse.bass as bass
from concourse import mybir

F32 = mybir.dt.float32
F32R = mybir.dt.float32r
U32 = mybir.dt.uint32
ALU = mybir.AluOpType
ACT = mybir.ActivationFunctionType
AX = mybir.AxisListType

B, S, D, H, DH = 4, 512, 256, 16, 128
NU = B * H
NG = 4
HID = [128, 256, 384, 512, 128, 256, 384, 512]
NC = sum(HID) // 128
EXPERT = [e for e, h in enumerate(HID) for _ in range(h // 128)]
LAG = 3
EULER = 2.718281828459045
WARM = 56, 4, 18
INV = 1.0 / float(DH) ** 0.5
BIG = 3.0e38

F_W1, F_DOWN, F_CORE, F_SH1, F_SH2, F_UP, F_RT = 0, 2560, 2816, 3328, 3456, 3584, 3840
F_END = 3856
W2_END = NC * 128
C_ID, C_MASK, C_EXM, C_IOTA, C_COST, C_RB, C_ONE, C_END = 0, 128, 640, 800, 808, 816, 824, 832
B_DOWN, B_SH1, B_B1, B_SH2, B_END = 0, 1, 2, 22, 23

P_OFF = [0, 128, 384, 768]
S_AT = [(1, 0), (2, 256), (1, 128), (0, 0)]
S_ORDER = [(1, [0, 2]), (0, [3]), (2, [1])]
T_OFF = [0, 512, 1024, 896]
T_AT = [0, 0, 0, 384]
T_COLS = {0: (0, 512), 1: (512, 1024), 2: (1024, 1280)}
T_ORDER = [(2, [2]), (1, [1, 3]), (0, [0])]


def unit(u):
    return u // 16, (u % 16) // 4, u % 4


def attention_plan():
    pre, post = {}, {}
    fill = {}

    def put(where, i, *events):
        where.setdefault(i, []).extend(events)

    put(post, 0, ("mg",))
    put(post, 1, ("ms",))
    for b in (1, 2, 3):
        i = (0, 3, 6)[b - 1]
        fill[i] = [[("st", b, 0)], [("st", b, 1)], [("st", b, 2)], [("st", b, 3)]]
        fill[i + 1] = [[("nm", b, 0)], [("nm", b, 1)]]
        put(post, i + 1, ("h", b, 0))
        put(post, i + 1 + (b > 1), ("h", b, 1))
    for n in range(4, 16):
        put(pre, 16 * (n // 4 - 1) + 5 + 2 * (n % 4), ("wh", n))
    for n in range(16, 20):
        put(pre, 34 + n, ("wh", n))
    fill[20] = [[("d0", 0)], [("d0", 1)], [], [], [("d0", 2)]]
    for b in range(2):
        fill[54 + 4 * b] = [[("st", B + b, k)] for k in range(4)]
        fill[55 + 4 * b] = [[("nm", B + b, 0)], [("nm", B + b, 1)]]
        put(post, 55 + 4 * b, ("h2", b, 0))
        put(post, 56 + 4 * b, ("h2", b, 1))
        put(post, 57 + 4 * b, ("r", b))
    fill[58] = [[("rs", 0, 1), ("rs", 0, 2)]] + fill[58]
    put(post, 58, *[("rp", 0, c) for c in range(4)])
    fill[59] += [[], [("rs", 0, 3)], [("rs", 0, 4)]]
    fill[60] = [[("rs", 0, k)] for k in range(5, 10)]
    fill[61] = [[("rs", 0, k)] for k in range(10, 15)]
    put(post, 61, ("wt", 0))
    fill[62] = [[("st", 6, 0), ("st", 6, 1)], [("st", 6, 2)], [("st", 6, 3)], [("nm", 6, 0), ("nm", 6, 1)]]
    put(post, 61, ("wh", 20))
    plan = [("b1",), ("mod0",)] + [("st", 0, k) for k in range(4)] + [("silu",), ("wh", 0), ("wh", 1),
            ("nm", 0, 0), ("nm", 0, 1), ("mod",),
            ("h", 0, 0), ("h", 0, 1), ("wh", 2), ("q", 0), ("k", 0), ("v", 0, 0), ("S", 0), ("norm", 0), ("q", 1), ("k", 1), ("v", 0, 1), ("T", 0), ("wh", 3)]
    for i in range(NU):
        steps = list(fill.get(i, []))

        def add(*events):
            for ev in events:
                plan.append(ev)
                if steps and ev[0] in ("S", "q", "wo", "z", "v", "T"):
                    plan.extend(steps.pop(0))

        if i + 1 < NU:
            add(("S", i + 1))
        if i + 2 < NU:
            add(("q", i + 2), ("k", i + 2))
        if i + 1 < NU:
            add(("norm", i + 1))
        if i >= 2:
            add(("wo", i // 2 - 1, i % 2))
        add(*pre.get(i, []))
        add(("z", i))
        if i + 2 < NU:
            add(("v", i // 2 + 1, i % 2))
        if i + 1 < NU:
            add(("T", i + 1))
        plan += [ev for group in steps for ev in group]
        plan += post.get(i, [])
        if i + 2 == NU:
            plan.append(("dn", 0))
    return plan


def ffn_plan():
    last = NU // 2 - 1
    at = {}

    def put(t, j, *events):
        at.setdefault((t, j), []).extend(events)

    put(0, 0, ("wh", 21))
    put(0, 0, ("rs", 1, 1))
    put(0, 1, ("rs", 1, 2), ("wo", last, 0))
    put(0, 2, ("wo", last, 1), ("wl", 0), ("wl", 1))
    put(0, 3, ("wh", 22))
    put(0, 4, ("h2", 2, 0))
    put(0, 5, ("h2", 2, 1), ("wl", 2), ("wl", 3))
    for k, j in enumerate((6, 7, 8, 9)):
        put(0, j, ("st", 7, k))
    for c in range(3):
        put(0, 9 + c, ("dta", c))
    put(0, 12, ("dt",), ("nm", 7, 0))
    put(0, 14, ("nm", 7, 1))
    put(0, 16, ("h2", 3, 0))
    put(0, 16, ("hs", 0, 0))
    put(0, 17, ("h2", 3, 1))
    put(0, 17, ("dn", 1))
    put(0, 18, ("gx", 0, 0), ("hs", 0, 1))
    put(0, 20, ("gx", 0, 1))
    put(1, 6, ("D", 0))
    for b, n in ((1, 5), (2, 26), (3, 47)):
        def at_(i, *events):
            put(*divmod(i, NC + 1), *events)
        if b > 1:
            at_(n, ("r", b))
            at_(n + 1, ("rs", b, 1), ("rs", b, 2))
        for c in range(4):
            at_(n + 2 + 2 * c, ("rp", b, c))
        for k in range(3, 10):
            at_(n + 9 + (k - 3) // 3, ("rs", b, k))
        for k in range(10, 15):
            at_(n + 13 + (k - 10) // 3, ("rs", b, k))
        at_(n + 17 - (b == 1), ("wt", b))
    for t in range(1, B):
        put(t, 2, ("xb", t - 1))
        put(t, 3, ("D", t))
        put(t, 6, ("o", t - 1), ("hs", t, 0))
        put(t, 8, ("gx", t, 0), ("hs", t, 1), ("up", t - 1, 0))
        put(t, 10, ("gx", t, 1), ("up", t - 1, 1))
        if t + 1 < B:
            put(t, 17, ("dn", t + 1))
    put(B - 1, 18, ("xb", B - 1))
    chunks = B * (NC + 1)
    plan, later = [], []
    for n in range(chunks + LAG):
        if n < chunks:
            plan.append(("w1", n))
        if n >= LAG:
            plan.append(("w2", n - LAG))
        plan += at.get(divmod(n, NC + 1), [])
        if n >= LAG and EXP_OF(n - LAG) != EXP_OF(n - LAG + 1):
            t, e = EXP_OF(n - LAG)
            plan.append(("acc", t, e))
            if e and 8 * t + e + 3 < 8 * B:
                later.append(8 * t + e + 3)
        while later and (later[0] < 8 or ("wt", later[0] // 8) in plan):
            plan.append(("wl", later.pop(0)))
    plan += [("o", B - 1), ("up", B - 1, 0), ("up", B - 1, 1)]
    return plan


def EXP_OF(n):
    t, j = divmod(n, NC + 1)
    return t, (0 if j == 0 else 1 + EXPERT[j - 1])


MISC = {"h": True, "q": True, "k": True, "v": True, "z": True, "wo": False, "h2": True, "r": False,
        "dn": True, "up": False, "wt": False, "D": False, "mg": False, "ms": False, "dt": False}
BY_V = (0, 21, 22)
OWN = [("acc", B - 1, 8)]


def build(nc, x, ct, wmod, wat, wfa, wfb, cst, bcol, b2, ub, cb, out, scr, scw):
    plan = attention_plan() + ffn_plan()
    use, rd = {}, {}
    for ev in plan:
        if ev[0] in MISC:
            use[ev] = len(use)
            if MISC[ev[0]]:
                rd[ev] = len(rd)
    accs = [ev for ev in plan if ev[0] in ("acc",)]
    acc_no = {ev[1:]: n for n, ev in enumerate(accs)}
    last_chunk = {}
    first_chunk = {}
    for n in range(B * (NC + 1)):
        last_chunk[EXP_OF(n)] = n
        first_chunk.setdefault(EXP_OF(n), n)

    wo_before = {}
    for ev in plan:
        if ev[0] in ("h", "h2"):
            wo_before[ev] = sum(1 for w in plan[:plan.index(ev)] if w[0] == "wo")

    with ExitStack() as ctx:
        def sb(name, cols, dt=F32, parts=128):
            return ctx.enter_context(nc.sbuf_tensor(name, [parts, cols], dt))

        def sem(name):
            return ctx.enter_context(nc.semaphore(name))

        hh, hl = sb("hh", 4096, F32R), sb("hl", 4096, F32R)
        W = [sb("W0", 8192, F32R), sb("W1", 8192, F32R)]
        X = sb("X", 4096)
        tmp = sb("tmp", 1024)
        fb = sb("fb", 1024)
        stage = sb("stage", 2048)
        cc = sb("cc", C_END)
        gab = sb("gab", 2048)
        bc = sb("bc", B_END)
        rows = sb("rows", 128 + 1024, parts=8)
        oub = sb("oub", 256)
        modt = sb("modt", 32)
        sil = sb("sil", 24)
        mv = sb("mv", 8 + 24)
        rs = sb("rs", 16)
        sm = sb("sm", 4)
        nb = sb("nb", 4)
        ri = sb("ri", 4)
        wg = sb("wg", 128)
        rt = sb("rt", 256)
        ebase = sb("ebase", 32)
        ru = sb("ru", 32, U32)
        g0 = sb("g0", 20 + 160 + 8)
        Dz = sb("Dz", 128, mybir.dt.bfloat16)
        Dm = sb("Dm", 128, parts=8)
        g0z = sb("g0z", 320, F32R)
        with ExitStack() as att:
            def sa(name, cols, dt=F32):
                return att.enter_context(nc.sbuf_tensor(name, [128, cols], dt))

            vh, vl = sa("vh", 2048, F32R), sa("vl", 2048, F32R)
            qk = sa("qk", 2048, F32R)
            zt = sa("zt", 4096, F32R)
            pth, ptl = sa("pth", 1280, F32R), sa("ptl", 1280, F32R)
            PB = sa("PB", 1280)
        Gr = sb("Gr", 4096, F32R)
        ur = sb("ur", 2048, F32R)
        gxh, gxl = sb("gxh", 2048, F32R), sb("gxl", 2048, F32R)
        oh, ol = sb("oh", 512, F32R), sb("ol", 512, F32R)
        prod = sb("prod", 1024)
        gob = sb("gob", 256)
        G32 = sb("G32", 1024)
        u0 = sb("u0", 512)

        PS = [ctx.enter_context(nc.psum_tensor(f"S{n}", [128, 512], F32)) for n in range(3)]
        PT = [ctx.enter_context(nc.psum_tensor(f"T{n}", [128, 512], F32)) for n in range(2)] + [PS[2]]
        M = [ctx.enter_context(nc.psum_tensor(f"M{n}", [128, 512], F32)) for n in range(3)]

        ident = cc[:, C_ID:C_ID + 128]
        mask = cc[:, C_MASK:C_MASK + 512]

        s_x = [sem(f"s_x{b}") for b in range(B)]
        s_ct, s_wm, s_wm2, s_c, s_b, s_bc, s_g = (sem(n) for n in ("s_ct", "s_wm", "s_wm2", "s_c", "s_b", "s_bc", "s_g"))
        s_st = [sem("s_st0"), sem("s_st1")]
        s_wh, s_wl, s_wd = sem("s_wh"), sem("s_wl"), sem("s_wd")
        s_sil, s_mod, s_mc, s_gr, s_gd = (sem(n) for n in ("s_sil", "s_mod", "s_mc", "s_gr", "s_gd"))
        mf, mh, me = sem("mf"), sem("mh"), sem("me")
        s_S, s_M, s_E, s_N, s_T = (sem(n) for n in ("s_S", "s_M", "s_E", "s_N", "s_T"))
        s_ph, s_pl = sem("s_ph"), sem("s_pl")
        s_v, s_a, s_mh = sem("s_v"), sem("s_a"), sem("s_mh")
        s_ve, s_r0, s_xn = sem("s_ve"), sem("s_r0"), sem("s_xn")
        s_le = sem("s_le")
        s_f1, s_gh, s_gl, s_o, s_ac = (sem(n) for n in ("s_f1", "s_gh", "s_gl", "s_o", "s_ac"))
        s_y, s_hs, s_xg, s_xl = (sem(n) for n in ("s_y", "s_hs", "s_xg", "s_xl"))
        s_g0, s_gz, s_dt, s_dc = (sem(n) for n in ("s_g0", "s_gz", "s_dt", "s_dc"))
        s_z = sem("s_z")
        s_xb = sem("s_xb")
        s_id = sem("s_id")
        s_ri, s_P3, s_rt, s_st_ = sem("s_ri"), sem("s_P3"), sem("s_rt"), sem("s_st_")
        s_ob, s_d0 = sem("s_ob"), sem("s_d0")
        s_pa, s_oc = sem("s_pa"), sem("s_oc")
        s_ws = [sem(f"s_ws{t}") for t in range(B)]
        s_wb = [sem(f"s_wb{n}") for n in range(4)]
        s_fin, s_out = sem("s_fin"), sem("s_out")

        def bank(ev):
            return M[use[ev] % 3]

        def hT(b, k):
            s = slice(b * 1024 + k * 512, b * 1024 + k * 512 + 512)
            return hh[:, s], hl[:, s]

        def hTc(b, k, c):
            s = slice(b * 1024 + k * 512 + c * 128, b * 1024 + k * 512 + c * 128 + 128)
            return hh[:, s], hl[:, s]

        def wt(slot, at, n):
            return W[slot][:, at:at + n], W[slot][:, 4096 + at:4096 + at + n]

        def zs(h):
            return zt[:, h * 1024:h * 1024 + 512], zt[:, h * 1024 + 512:h * 1024 + 1024]

        def u_at(t):
            o = (t % 2) * 1024
            return ur[:, o:o + 512], ur[:, o + 512:o + 1024]

        def gx_at(t, k):
            o = (t % 2) * 1024 + k * 512
            return gxh[:, o:o + 512], gxl[:, o:o + 512]

        def u32(t):
            return u0[:]

        def acc_at(t):
            return stage[:, 1024 + (t % 2) * 512:1536 + (t % 2) * 512]

        def Gs(n):
            o = (n % 4) * 1024
            return Gr[:, o:o + 512], Gr[:, o + 512:o + 1024]

        def wb_at(i):
            o = (i % 2) * 512
            return (gab if i % 4 < 2 else tmp)[:, o:o + 512]

        def wT(t):
            return rows[0:8, 128 + (t % 2) * 512:640 + (t % 2) * 512]

        def xn_at(ev):
            return stage[:, 0:1024] if ev[:2] == ("h2", 3) else tmp[:]

        def lane(pair, a, n):
            return pair[0][:, a:a + n], pair[1][:, a:a + n]

        def piece(n):
            if n < 16:
                return wat[n // 4][:, (n % 4) * 1024:(n % 4) * 1024 + 1024], (n // 4) % 2, (n % 4) * 1024, 1024
            if n < 20:
                a = (n - 16) * 1024
                w = min(1024, F_END - a)
                return wfa[:, a:a + w], 0, a, w
            a = (n - 20) * 1024
            w = min(1024, W2_END - a)
            return wfb[:, a:a + w], 1, a, w

        def piece_after(n):
            if n < 8:
                return None
            if n < 20:
                return ("wo", 8 * (n // 4) - 9, 1)
            return ("v", NU // 2 - 1, 1)

        block = ctx.enter_context(nc.Block())

        @block.sync
        def _(sp):
            def load(n):
                src, _, _, w = piece(n)
                sp.dma_start(stage[:, (n % 2) * 1024:(n % 2) * 1024 + w], src).then_inc(s_st[n % 2], 16)

            def load_x(b):
                sp.dma_start(X[:, b * 1024:b * 1024 + 1024], x[:, b * 1024:b * 1024 + 1024]).then_inc(s_x[b], 16)

            load_x(0)
            load(0)
            sp.dma_start(cc[:, 0:128], cst[:, 0:128]).then_inc(s_id, 16)
            load(1)
            sp.dma_start(cc[:, 128:], cst[:, 128:]).then_inc(s_c, 16)
            for ev in plan:
                if ev[0] == "ms":
                    sp.wait_ge(mf, use[ev] + 1)
                    load_x(2)
                    load_x(3)
                elif ev[0] == "wh":
                    n = ev[1]
                    if n == 2:
                        sp.dma_start(X[:, 2048:4096], wmod[:, 1024:3072]).then_inc(s_wm2, 16)
                        load_x(1)
                    if n + 2 < 23:
                        sp.wait_ge(s_wl, n) if n else sp.wait_ge(s_wd, 1)
                        load(n + 2)
                elif ev[0] == "wt":
                    t = ev[1]
                    sp.wait_ge(me, use[ev] + 1)
                    sp.dma_start(scw[8 * t:8 * t + 8, :], wT(t)).then_inc(s_ws[t], 16)
                elif ev[0] == "wl":
                    i = ev[1]
                    sp.wait_ge(s_ws[i // 8], 16)
                    if i < 2:
                        sp.wait_ge(me, use[("wo", NU // 2 - 1, 1)] + 1)
                    elif i < 4:
                        sp.wait_ge(mf, use[("h2", 2, 1)] + 1)
                    else:
                        sp.wait_ge(s_ac, acc_no[divmod(i - 4, 8)[0], (i - 4) % 8 + 1] + 1)
                    sp.dma_start(wb_at(i), scw[i:i + 1, :].broadcast_to([128, 512])).then_inc(s_wb[i % 4], 16)
                elif ev[0] == "up" and (ev[2] == 1 or ev[1] == B - 1):
                    _, t, c = ev
                    sp.wait_ge(s_fin, 2 * t + c + 1)
                    s = slice(t * 1024 + 512 * c * (t == B - 1), t * 1024 + 512 * (c + 1))
                    sp.dma_start(out[:, s], X[:, s]).then_inc(s_out, 16)
            sp.wait_ge(s_out, 16 * (B + 1))

        @block.gpsimd
        def _(pool):
            pool.memset(rs[:, 12:16], -0.5).then_inc(s_mh, 1)
            pool.memset(ebase[:], float(EULER)).then_inc(s_mh, 1)
            pool.dma_start(bc[:], bcol).then_inc(s_bc, 16)
            pool.dma_start(rows[:, 0:128], b2).then_inc(s_b, 16)
            pool.dma_start(oub[:], ub.broadcast_to([128, 256])).then_inc(s_b, 16)
            pool.dma_start(gab[:, 0:256], cb.broadcast_to([128, 256])).then_inc(s_b, 16)
            ln_no = 0
            for ev in plan:
                if ev[0] == "st" and ev[2] == 3:
                    if ln_no == 0:
                        pool.wait_ge(s_mh, 2)
                    pool.wait_ge(s_ve, ln_no + 1)
                    pool.tensor_tensor(rs[:, 4:8], rs[:, 0:4], rs[:, 12:16], ALU.pow).then_inc(s_r0, 1)
                    ln_no += 1
                if ev[0] == "mg":
                    rg, g1, g2 = rows[0:4, 640:1152], gab[0:4, 0:512], gab[0:4, 512:1024]
                    pool.wait_ge(s_ob, 2)
                    pool.wait_ge(me, use[ev] + 1)
                    pool.tensor_scalar(g2, rg, 0.0, 2.0, ALU.is_ge, ALU.mult).then_inc(s_gr, 1)
                    pool.wait_ge(s_gr, 1)
                    pool.tensor_scalar(g2, g2, -1.0, None, ALU.add).then_inc(s_gr, 1)
                    pool.wait_ge(s_gr, 2)
                    pool.tensor_tensor(g1, rg, g2, ALU.mult).then_inc(s_gr, 1)
                    pool.wait_ge(s_gr, 3)
                    pool.tensor_scalar(g1, g1, 0.25, None, ALU.max).then_inc(s_gr, 1)
                    pool.wait_ge(s_gr, 4)
                    pool.tensor_tensor(rg, g1, g2, ALU.mult).then_inc(s_gr, 1)
                    pool.wait_ge(s_gr, 5)
                    for n in range(2):
                        pool.dma_start(scr[n], rows[0:4, 640 + 256 * n:896 + 256 * n]).then_inc(s_gd, 16)
                    pool.wait_ge(s_gd, 32)
                    flat = scr.rearrange("(o a) b n -> o (a b n)", o=1)
                    pool.dma_start(gab[:], flat.broadcast_to([128, 2048])).then_inc(s_g, 16)
                if ev[0] == "acc" and ev[2] > 0 and ev not in OWN:
                    _, t, e = ev
                    i = 8 * t + e - 1
                    pool.wait_ge(s_ac, acc_no[(t, e)] + 1)
                    pool.wait_ge(s_pa, i) if i else None
                    pool.tensor_tensor(acc_at(t), acc_at(t), prod[:, (i % 2) * 512:(i % 2) * 512 + 512],
                                       ALU.add).then_inc(s_pa, 1)
                if ev[0] == "rp" or (ev[0] == "rs" and ev[2] == 9):
                    pool.wait_ge(s_rt, 15 * ev[1] + (3 if ev[0] == "rp" else 10))
                    if ev[0] == "rp":
                        w, dst, src = 8, rt[:, 64 + 8 * ev[2]:72 + 8 * ev[2]], rt[:, 32 + 8 * ev[2]:40 + 8 * ev[2]]
                    else:
                        w, dst, src = 4, rt[:, 168:172], rt[:, 160:164]
                    pool.tensor_tensor(dst, ebase[:, 0:w], src, ALU.pow).then_inc(s_le, 1)
                if ev[0] == "wh" and ev[1] not in BY_V:
                    n = ev[1]
                    _, slot, a, w = piece(n)
                    hi, lo = wt(slot, a, w)
                    pool.wait_ge(s_wh, n + 1)
                    pool.tensor_tensor(lo, stage[:, (n % 2) * 1024:(n % 2) * 1024 + w], hi.bitcast(F32),
                                       ALU.subtract).then_inc(s_wl, 1)
                if ev[0] == "wo":
                    _, p, c2 = ev
                    a = unit(2 * p)[1] * 1024 + c2 * 512
                    pool.wait_ge(me, use[ev] + 1)
                    if p:
                        pool.wait_ge(s_y, 2 * p + c2 - 1)
                    pool.tensor_tensor(X[:, a:a + 512], X[:, a:a + 512], fb[:, c2 * 512:c2 * 512 + 512],
                                       ALU.add).then_inc(s_y, 1)
                if ev[0] == "hs":
                    _, t, k = ev
                    pool.wait_ge(me, use[("h2", t, 1)] + 1)
                    pool.wait_ge(mf, use[("h2", 3, 1)] + 1)
                    a, l = hT(t, k)
                    pool.wait_ge(s_xg, 2 * t + k)
                    pool.tensor_tensor(stage[:, 0:512], a.bitcast(F32), l.bitcast(F32), ALU.add).then_inc(s_hs, 1)
                if ev[0] == "xb":
                    t = ev[1]
                    g = gab[:, 1024 + t * 256:1280 + t * 256]
                    if t:
                        pool.wait_ge(s_xb, 2 * t)
                    pool.wait_ge(s_xn, 2 * (B + t) + 2)
                    pool.wait_ge(s_g, 16)
                    pool.tensor_tensor(gob[:], oub[:], g, ALU.mult).then_inc(s_xb, 1)
                    pool.wait_ge(s_xb, 2 * t + 1)
                    y = X[:, t * 1024:t * 1024 + 1024].rearrange("p (a n) -> p a n", a=4)
                    gg = gob[:].rearrange("p (a n) -> p a n", a=1)
                    pool.tensor_tensor(y, y, gg.broadcast_to([128, 4, 256]), ALU.add).then_inc(s_xb, 1)
                if ev[0] == "up" and ev[1] < B - 1:
                    _, t, c = ev
                    y = X[:, t * 1024 + c * 512:t * 1024 + c * 512 + 512]
                    pool.wait_ge(s_xb, 2 * t + 2)
                    pool.wait_ge(me, use[ev] + 1)
                    pool.tensor_tensor(y, y, fb[:, c * 512:c * 512 + 512], ALU.add).then_inc(s_fin, 1)

        @block.scalar
        def _(act):
            act.dma_start(sil[:, 0:8], ct).then_inc(s_ct, 16)
            act.dma_start(PB[:, 0:1024], wmod[:, 0:1024]).then_inc(s_wm, 16)

            fb_held = [0, 0]

            def exps(u, ns):
                for n in ns:
                    bk, chunks = S_ORDER[n]
                    act.wait_ge(s_M, 3 * u + n + 1)
                    if u > 0 and n == 0:
                        act.wait_ge(s_N, u)
                    for i in chunks:
                        w = 128 * (i + 1)
                        a = S_AT[i][1]
                        ins = act.activation(PB[:, P_OFF[i]:P_OFF[i] + w], PS[bk][:, a:a + w], ACT.Exp,
                                             bias=nb[:, i:i + 1], scale=-1.0, accum_out=sm[:, i:i + 1])
                    ins.then_inc(s_E, 1)

            for ev in plan:
                kind = ev[0]
                if kind == "mod0":
                    act.wait_ge(s_ct, 16)
                    act.activation(sil[:, 8:16], sil[:, 0:8], ACT.Exp, scale=-1.0).then_inc(s_sil, 1)
                elif kind == "b1":
                    act.wait_ge(s_bc, 16)
                    act.activation(g0[:, 0:20], bc[:, B_B1:B_B1 + 20], ACT.Gelu).then_inc(s_g0, 1)
                elif kind == "wh":
                    n = ev[1]
                    _, slot, a, w = piece(n)
                    act.wait_ge(s_st[n % 2], 16 * (n // 2 + 1))
                    if piece_after(n):
                        act.wait_ge(mf, use[piece_after(n)] + 1)
                    act.copy(wt(slot, a, w)[0], stage[:, (n % 2) * 1024:(n % 2) * 1024 + w]).then_inc(s_wh, 1)
                elif kind in ("h", "h2"):
                    _, b, k = ev
                    o = 0 if kind == "h" else 16
                    act.wait_ge(mf, use[ev] + 1)
                    if use[ev] == 0:
                        act.wait_ge(s_mc, 1)
                    act.wait_ge(s_y, wo_before[ev])
                    if fb_held[k]:
                        act.wait_ge(me, fb_held[k])
                    fb_held[k] = use[ev] + 1
                    bias = modt[:, o + 4 * k + b:o + 4 * k + b + 1]
                    scale = modt[:, o + 8 + 4 * k + b:o + 9 + 4 * k + b]
                    if ev[:2] != ("h", 0):
                        act.activation(fb[:, 512 * k:512 * k + 512], bank(ev)[:], ACT.Identity, bias=bias,
                                       scale=scale).then_inc(s_v, 1)
                    act.activation(hT(b, k)[0], bank(ev)[:], ACT.Identity, bias=bias, scale=scale).then_inc(mh, 1)
                elif kind == "norm":
                    u = ev[1]
                    act.wait_ge(s_ri, u + 1)
                    p = PB[:, P_OFF[3]:P_OFF[3] + 512]
                    act.activation(p, p, ACT.Copy, scale=ri[:, 3:4]).then_inc(s_P3, 1)
                elif kind in ("q", "k", "v", "z"):
                    act.wait_ge(mf, use[ev] + 1)
                    if kind == "q":
                        dst = qk[:, 0:512]
                    elif kind == "k":
                        dst = qk[:, 1024:1536]
                    elif kind == "v":
                        o = (ev[1] % 2) * 1024 + ev[2] * 512
                        dst = vh[:, o:o + 512]
                    else:
                        dst = zs(ev[1] % 4)[0]
                    act.copy(dst, bank(ev)[:]).then_inc(mh, 1)
                    if kind == "q" and ev[1] >= 2:
                        exps(ev[1] - 1, [1, 2])
                elif kind == "S":
                    u = ev[1]
                    exps(u, [0] if 1 <= u < NU - 1 else [0, 1, 2])
                elif kind == "T":
                    u = ev[1]
                    for n, (bk, _) in enumerate(T_ORDER):
                        a, z = T_COLS[bk]
                        act.wait_ge(s_T, 3 * u + n + 1)
                        act.copy(pth[:, a:z], PT[bk][:, 0:z - a]).then_inc(s_ph, 1)
                elif kind == "dn":
                    t = ev[1]
                    act.wait_ge(mf, use[ev] + 1)
                    if t == 0:
                        act.wait_ge(s_T, 3 * NU)
                    else:
                        act.wait_ge(me, use[("dn", t - 1)] + 1)
                    act.activation(u32(t), bank(ev)[:], ACT.Gelu,
                                   bias=bc[:, B_DOWN:B_DOWN + 1]).then_inc(s_v, 1)
                    act.activation(u_at(t)[0], bank(ev)[:], ACT.Gelu,
                                   bias=bc[:, B_DOWN:B_DOWN + 1]).then_inc(mh, 1)
                elif kind == "gx":
                    _, t, k = ev
                    act.wait_ge(s_xl, 2 * t + k)
                    if t >= 2:
                        act.wait_ge(mf, use[("up", t - 2, 1)] + 1)
                    act.wait_ge(s_hs, 2 * t + k + 1)
                    act.activation(stage[:, 512:1024], stage[:, 0:512], ACT.Gelu).then_inc(s_v, 1)
                    act.activation(gx_at(t, k)[0], stage[:, 0:512], ACT.Gelu).then_inc(s_xg, 1)
                elif kind == "w1":
                    n = ev[1]
                    t, j = divmod(n, NC + 1)
                    bias = bc[:, B_SH1:B_SH1 + 1] if j == 0 else bc[:, B_B1 + j - 1:B_B1 + j]
                    act.wait_ge(s_f1, n + 1)
                    act.wait_ge(s_gl, n - 1) if n >= 2 else None
                    act.activation(G32[:, (n % 2) * 512:(n % 2) * 512 + 512], PS[n % 3][:], ACT.Gelu,
                                   bias=bias).then_inc(s_v, 1)
                    act.activation(Gs(n)[0], PS[n % 3][:], ACT.Gelu, bias=bias).then_inc(s_gh, 1)

        @block.tensor
        def _(pe):
            def mm3(o, lhs, rhs, start, stop, **kw):
                pe.matmul(o, lhs[0], rhs[0], start=start, stop=False, **kw)
                pe.matmul(o, lhs[0], rhs[1], start=False, stop=False, **kw)
                return pe.matmul(o, lhs[1], rhs[0], start=False, stop=stop, **kw)

            pe.wait_ge(s_z, 1)

            def warm(n):
                for _ in range(n):
                    pe.matmul(PT[0][:, 0:128], Dz[:], Dz[:], start=True, stop=True)

            warm(WARM[0])
            ln_no = 0
            for ev in plan:
                kind = ev[0]
                if kind in MISC:
                    m = use[ev]
                    o = bank(ev)
                    if m >= 3:
                        pe.wait_ge(me, m - 2)
                if kind == "mod":
                    pe.wait_ge(s_wm, 16)
                    pe.wait_ge(s_sil, 2)
                    wm = PB[:, 0:1024].rearrange("p (k n) -> p k n", k=2)
                    sl = sil[:, 16:24].rearrange("p (k n) -> p k n", k=2)
                    for n in range(4):
                        for k in range(2):
                            ins = pe.matmul(PS[0][:, 4 * n:4 * n + 4], wm[:, k, 128 * n:128 * n + 128], sl[:, k, :],
                                            start=(k == 0), stop=(k == 1))
                    ins.then_inc(s_mod, 1)
                    warm(WARM[1])
                elif kind == "mg":
                    pe.wait_ge(s_wm2, 16)
                    wm = X[:, 2048:4096].rearrange("p (k n) -> p k n", k=2)
                    for k in range(2):
                        ins = pe.matmul(o[0:4, :], sl[:, k, :], wm[:, k, 0:512], start=(k == 0), stop=(k == 1))
                    ins.then_inc(mf, 1)
                elif kind == "ms":
                    for n in range(4):
                        for k in range(2):
                            ins = pe.matmul(o[:, 4 * n:4 * n + 4], wm[:, k, 512 + 128 * n:640 + 128 * n],
                                            sl[:, k, :], start=(k == 0), stop=(k == 1))
                    ins.then_inc(mf, 1)
                elif kind in ("h", "h2"):
                    _, b, k = ev
                    if k == 0:
                        pe.wait_ge(s_xn, 2 * ln_no + 2)
                        ln_no += 1
                    if m == 0:
                        pe.wait_ge(s_id, 16)
                    for c in range(4):
                        ins = pe.transpose(o[:, 128 * c:128 * c + 128],
                                           xn_at(ev)[:, 256 * c + 128 * k:256 * c + 128 * k + 128], ident)
                    ins.then_inc(mf, 1)
                    if ev == ("h", 0, 1):
                        warm(WARM[2])
                elif kind in ("q", "k"):
                    g, b, h = unit(ev[1])
                    if h == 0:
                        pe.wait_ge(me, use[("h", b, 0)] + 1)
                        pc = 4 * g + (kind == "k")
                        pe.wait_ge(s_wl, pc) if pc else pe.wait_ge(s_wd, 1)
                    a = (kind == "k") * 1024 + h * 128
                    for k in range(2):
                        if k and h == 0:
                            pe.wait_ge(me, use[("h", b, 1)] + 1)
                        ins = mm3(o[:], wt(g % 2, a + 512 * k, 128), hT(b, k), k == 0, k == 1)
                    ins.then_inc(mf, 1)
                elif kind == "v":
                    _, p, c2 = ev
                    g, b, h = unit(2 * p)
                    pe.wait_ge(s_wl, 4 * g + 2)
                    for c in range(2):
                        for k in range(2):
                            ins = mm3(o[:, 256 * c:256 * c + 256], hTc(b, k, 2 * c2 + c),
                                      wt(g % 2, 2048 + 512 * k + 128 * h, 256), k == 0, k == 1)
                    ins.then_inc(mf, 1)
                elif kind == "S":
                    u = ev[1]
                    pe.wait_ge(me, use[("k", u)] + 1)
                    if u == 0:
                        pe.wait_ge(s_mc, 1)
                    q = (qk[:, 0:512], qk[:, 512:1024])
                    kk = (qk[:, 1024:1536], qk[:, 1536:2048])
                    for n, (bk, chunks) in enumerate(S_ORDER):
                        if u > 0:
                            pe.wait_ge(s_E, 3 * u - 3 + n + 1)
                            if bk == 2:
                                pe.wait_ge(s_pl, 3 * u - 2)
                        for i in chunks:
                            a, w = S_AT[i][1], 128 * (i + 1)
                            ins = mm3(PS[bk][:, a:a + w], lane(q, 128 * i, 128), lane(kk, 0, w), True, True)
                        ins.then_inc(s_S, 1)
                elif kind == "T":
                    u = ev[1]
                    pe.wait_ge(s_N, u + 1)
                    pe.wait_ge(s_P3, u + 1)
                    for n, (bk, chunks) in enumerate(T_ORDER):
                        if u > 0:
                            pe.wait_ge(s_pl, 3 * u - 3 + n + 1)
                        for j in chunks:
                            a = T_AT[j]
                            for i in range(j, 4):
                                ins = pe.transpose(PT[bk][:, a + 128 * (i - j):a + 128 * (i - j) + 128],
                                                   PB[:, P_OFF[i] + 128 * j:P_OFF[i] + 128 * j + 128], ident)
                        ins.then_inc(s_T, 1)
                elif kind == "z":
                    u = ev[1]
                    h = u % 4
                    pe.wait_ge(me, use[("v", u // 2, 1)] + 1)
                    va = (u // 2 % 2) * 1024 + (u % 2) * 128
                    pe.wait_ge(s_pl, 3 * u + 3)
                    for j in range(4):
                        w = 512 - 128 * j
                        ins = mm3(o[:, 128 * j:512], (vh[:, va + 256 * j:va + 256 * j + 128],
                                                      vl[:, va + 256 * j:va + 256 * j + 128]),
                                  (pth[:, T_OFF[j]:T_OFF[j] + w], ptl[:, T_OFF[j]:T_OFF[j] + w]), j == 0, j == 3)
                    ins.then_inc(mf, 1)
                elif kind == "wo":
                    _, p, c2 = ev
                    g = unit(2 * p)[0]
                    pe.wait_ge(me, use[("z", 2 * p + 1)] + 1)
                    pe.wait_ge(s_wl, 4 * g + 3)
                    for c in range(2):
                        for n in range(2):
                            h = (2 * p + n) % 4
                            ins = mm3(o[:, 256 * c:256 * c + 256], lane(zs(h), 256 * c2 + 128 * c, 128),
                                      wt(g % 2, 3072 + 256 * h, 256), n == 0, n == 1)
                    ins.then_inc(mf, 1)
                elif kind == "r":
                    b = ev[1]
                    pe.wait_ge(s_wl, 19)
                    pe.wait_ge(me, use[("h2", b, 1)] + 1)
                    both = W[0][:].rearrange("p (a n) -> p a n", a=2)
                    for c in range(4):
                        oo = o[:, 16 * c:16 * c + 16].rearrange("p (a n) -> p a n", a=2)
                        for k in range(2):
                            l, w = hTc(b, k, c), both[:, :, F_RT + 8 * k:F_RT + 8 * k + 8]
                            pe.matmul(oo, l[0], w, start=(k == 0), stop=False)
                            ins = pe.matmul(oo, l[1], w, start=False, stop=(k == 1))
                    ins.then_inc(mf, 1)
                elif kind == "dn":
                    t = ev[1]
                    pe.wait_ge(s_wl, 19)
                    pe.wait_ge(me, use[("h2", t, 1)] + 1)
                    for k in range(2):
                        ins = mm3(o[:], wt(0, F_DOWN + 128 * k, 128), hT(t, k), k == 0, k == 1)
                    ins.then_inc(mf, 1)
                elif kind == "w1":
                    n = ev[1]
                    t, j = divmod(n, NC + 1)
                    if j == 0:
                        pe.wait_ge(me, use[("dn", t)] + 1)
                    if n >= 3:
                        pe.wait_ge(s_gh, n - 2)
                    else:
                        pe.wait_ge(s_E, 3 * NU)
                    a = F_SH1 if j == 0 else F_W1 + 128 * (j - 1)
                    mm3(PS[n % 3][:], wt(0, a, 128), u_at(t), True, True).then_inc(s_f1, 1)
                elif kind == "w2":
                    n = ev[1]
                    t, j = divmod(n, NC + 1)
                    X_ = acc_no[EXP_OF(n)]
                    first, last = first_chunk[EXP_OF(n)] == n, last_chunk[EXP_OF(n)] == n
                    pe.wait_ge(s_gl, n + 1)
                    if n == 0:
                        pe.wait_ge(s_pl, 3 * NU)
                    if t == 0 and j and (j - 1) % 8 == 0:
                        (pe.wait_ge(s_wl, 20) if j == 1 else pe.wait_ge(s_wd, 1 + (j - 1) // 8))
                    if first and X_ >= 2:
                        pe.wait_ge(s_ac, X_ - 1)
                    w = wt(0, F_SH2, 128) if j == 0 else wt(1, 128 * (j - 1), 128)
                    ins = mm3(PT[X_ % 2][:], w, Gs(n), first, last)
                    if last:
                        ins.then_inc(s_o, 1)
                elif kind == "dta":
                    o = bank(("dt",))
                    if ev[1] == 0:
                        pe.wait_ge(s_wd, 3)
                        pe.wait_ge(s_gz, 1)
                        pe.wait_ge(me, use[("dt",)] - 2)
                    for c in range(7 * ev[1], min(NC, 7 * ev[1] + 7)):
                        w = wt(1, 128 * c, 128)
                        g = g0z[:, 16 * c:16 * c + 16]
                        pe.matmul(o[:, 0:16], w[0], g, start=(c == 0), stop=False)
                        ins = pe.matmul(o[:, 0:16], w[1], g, start=False, stop=(c == NC - 1))
                    if ev[1] == 2:
                        ins.then_inc(s_dt, 1)
                elif kind == "dt":
                    pe.wait_ge(s_dc, 1)
                    pe.matmul(o[0:8, 128:256], g0[:, 180:188], ident, start=True, stop=False)
                    pe.matmul(o[0:8, 128:256], cc[0:8, C_ONE:C_ONE + 8], rows[0:8, 0:128],
                              start=False, stop=True).then_inc(mf, 1)
                elif kind == "wt":
                    t = ev[1]
                    pe.wait_ge(s_rt, 15 * t + 15)
                    for c in range(4):
                        ins = pe.transpose(o[0:8, 128 * c:128 * c + 128], wg[:, 32 * t + 8 * c:32 * t + 8 * c + 8],
                                           ident)
                    ins.then_inc(mf, 1)
                elif kind == "D":
                    t = ev[1]
                    pe.wait_ge(me, use[("wt", t)] + 1)
                    pe.wait_ge(me, use[("dt",)] + 1)
                    pe.matmul(o[:], Dm[0:8, :], wT(t), start=True, stop=True).then_inc(mf, 1)
                elif kind == "up":
                    _, t, c2 = ev
                    pe.wait_ge(s_xl, 2 * t + 2)
                    for c in range(2):
                        cx = 2 * c2 + c
                        oo = o[:, 256 * c:256 * c + 256]
                        for k in range(2):
                            mm3(oo, lane(gx_at(t, k), 128 * cx, 128), wt(0, F_CORE + 256 * k, 256), k == 0, False)
                        pe.wait_ge(s_oc, t + 1 + (c2 if t == B - 1 else 0))
                        ins = mm3(oo, lane((oh, ol), 128 * cx, 128), wt(0, F_UP, 256), False, True)
                    ins.then_inc(mf, 1)

        @block.vector
        def _(v):
            chain = [0]
            s_l = ctx.enter_context(nc.semaphore("s_l"))

            def link(ins):
                chain[0] += 1
                ins.then_inc(s_l, 1)
                v.wait_ge(s_l, chain[0])

            def bcast(ap, shape):
                return ap.broadcast_to(shape)

            def per(ap):
                return bcast(ap.rearrange("p (a n) -> p a n", n=1), [128, 4, 8])

            def router(ev, b, k):
                L, e0, pr = rt[:, 0:32], rt[:, 32:64], rt[:, 64:96]
                L3, e3, pr3 = (a.rearrange("p (a n) -> p a n", a=4) for a in (L, e0, pr))
                mx = rt[:, 96:100]
                ee, ga_, gb_ = rt[:, 168:172], rt[:, 172:176], rt[:, 176:180]
                rb, co, io = (cc[:, a:a + 8].rearrange("p (a n) -> p a n", a=1) for a in (C_RB, C_COST, C_IOTA))
                io4 = bcast(io, [128, 4, 8])
                top = [rt[:, 128 + 8 * c:136 + 8 * c] for c in range(4)]
                if k == 0:
                    v.wait_ge(mf, use[ev] + 1)
                    if b:
                        v.wait_ge(s_rt, 15 * b)
                    o = bank(ev)[:, 0:64].rearrange("p (a n) -> p a n", a=4)
                    link(v.tensor_tensor(L3, o[:, :, 0:8], bcast(rb, [128, 4, 8]), ALU.add))
                    v.tensor_tensor(L3, L3, o[:, :, 8:16], ALU.add).then_inc(me, 1)
                    v.wait_ge(me, use[ev] + 1)
                    return v.tensor_tensor(L3, L3, bcast(co, [128, 4, 8]), ALU.subtract)
                if k == 1:
                    return v.tensor_reduce(mx, L3, AX.X, ALU.max)
                if k == 2:
                    return v.tensor_tensor(e3, L3, per(mx), ALU.subtract)
                if k == 3:
                    v.wait_ge(s_le, 5 * b + 4)
                    return v.tensor_reduce(mx, pr3, AX.X, ALU.add)
                if k == 4:
                    return v.reciprocal(mx, mx)
                if k == 5:
                    return v.tensor_tensor(pr3, pr3, per(mx), ALU.mult)
                if k == 6:
                    for c in range(4):
                        ins = v.max(top[c], pr[:, 8 * c:8 * c + 8])
                    return ins
                if k == 7:
                    for c in range(4):
                        ins = v.max_index(ru[:, 8 * c:8 * c + 8], top[c], pr[:, 8 * c:8 * c + 8])
                    return ins
                if k == 8:
                    return v.tensor_copy(L, ru[:])
                if k == 9:
                    return v.tensor_tensor(rt[:, 160:164], rt[:, 129:160:8], rt[:, 128:160:8], ALU.subtract)
                if k == 10:
                    v.wait_ge(s_le, 5 * b + 5)
                    return v.tensor_scalar(ga_, ee, 1.0, None, ALU.add)
                if k == 11:
                    return v.reciprocal(ga_, ga_)
                if k == 12:
                    v.tensor_tensor(e3, io4, per(L[:, 0:32:8]), ALU.is_equal)
                    v.tensor_tensor(pr3, io4, per(L[:, 1:32:8]), ALU.is_equal)
                    return v.tensor_tensor(gb_, ga_, ee, ALU.mult)
                if k == 13:
                    v.tensor_tensor(e3, e3, per(ga_), ALU.mult)
                    return v.tensor_tensor(pr3, pr3, per(gb_), ALU.mult)
                return v.tensor_tensor(wg[:, 32 * b:32 * b + 32].rearrange("p (a n) -> p a n", a=4), e3, pr3, ALU.add)

            def silu():
                v.wait_ge(s_ct, 16)
                v.wait_ge(s_sil, 1)
                link(v.tensor_scalar(sil[:, 16:24], sil[:, 8:16], 1.0, None, ALU.add))
                link(v.reciprocal(sil[:, 16:24], sil[:, 16:24]))
                v.tensor_tensor(sil[:, 16:24], sil[:, 16:24], sil[:, 0:8], ALU.mult).then_inc(s_sil, 1)

            tmp_read = [use[("h", b, 1)] + 1 for b in range(B)] + [use[("h2", b, 1)] + 1 for b in range(B)]
            fb_held = [0, 0]
            xv = 0
            for ev in plan:
                kind = ev[0]
                if kind == "mod0":
                    v.memset(Dz[:], 0).then_inc(s_z, 1)
                elif kind == "mod":
                    v.wait_ge(s_mod, 1)
                    v.tensor_copy(modt[:, 0:8], PS[0][:, 0:8])
                    v.tensor_scalar(modt[:, 8:16], PS[0][:, 8:16], 1.0, None, ALU.add).then_inc(s_mc, 1)
                elif kind == "mg":
                    v.wait_ge(s_b, 48)
                    v.wait_ge(s_bc, 16)
                    v.tensor_tensor(oub[:], oub[:], gab[:, 0:256], ALU.add).then_inc(s_ob, 1)
                    v.tensor_scalar(bc[:, B_SH2:B_SH2 + 1], bc[:, B_SH2:B_SH2 + 1], 0.1, None, ALU.mult).then_inc(s_ob, 1)
                    v.wait_ge(mf, use[ev] + 1)
                    v.tensor_copy(rows[0:4, 640:1152], bank(ev)[0:4, :]).then_inc(me, 1)
                elif kind == "ms":
                    v.wait_ge(mf, use[ev] + 1)
                    v.tensor_copy(modt[:, 16:24], bank(ev)[:, 0:8])
                    v.tensor_scalar(modt[:, 24:32], bank(ev)[:, 8:16], 1.0, None, ALU.add).then_inc(me, 1)
                elif kind == "wh" and ev[1] in BY_V:
                    n = ev[1]
                    _, slot, a, w = piece(n)
                    hi, lo = wt(slot, a, w)
                    v.wait_ge(s_wh, n + 1)
                    v.tensor_tensor(lo, stage[:, (n % 2) * 1024:(n % 2) * 1024 + w], hi.bitcast(F32), ALU.subtract)\
                     .then_inc(s_wd, 1)
                elif kind == "silu":
                    silu()
                elif kind == "st":
                    _, n, k = ev
                    b = n % B
                    if k == 0:
                        if n < B:
                            v.wait_ge(s_x[b], 16)
                        else:
                            v.wait_ge(s_y, 2 * (25 + 2 * b) + 2)
                        if n:
                            v.wait_ge(s_xn, 2 * n)
                    if k < 2:
                        for c in (2 * k, 2 * k + 1):
                            ins = v.bn_stats(mv[:, 8 + 6 * c:14 + 6 * c], X[:, b * 1024 + 256 * c:b * 1024 + 256 * c + 256])
                        ins.then_inc(s_st_, 1)
                    elif k == 2:
                        v.wait_ge(s_st_, 3 * n + 2)
                        for c in range(4):
                            ins = v.bn_aggr(mv[:, 2 * c:2 * c + 2], mv[:, 8 + 6 * c:14 + 6 * c])
                        ins.then_inc(s_st_, 1)
                    else:
                        v.wait_ge(s_st_, 3 * n + 3)
                        v.tensor_scalar(rs[:, 0:4], mv[:, 1:8:2], 1e-5, None, ALU.add).then_inc(s_ve, 1)
                elif kind == "nm":
                    _, n, k = ev
                    b = n % B
                    dst = stage[:, 0:1024] if n == 7 else tmp[:]
                    if n == 7:
                        v.wait_ge(s_wd, 3)
                    elif n:
                        v.wait_ge(mf, tmp_read[n - 1])
                    v.wait_ge(s_r0, n + 1)
                    for c in (2 * k, 2 * k + 1):
                        ins = v.tensor_scalar(dst[:, 256 * c:256 * c + 256],
                                              X[:, b * 1024 + 256 * c:b * 1024 + 256 * c + 256],
                                              mv[:, 2 * c:2 * c + 1], rs[:, 4 + c:5 + c], ALU.subtract, ALU.mult)
                    ins.then_inc(s_xn, 1)
                elif kind in ("h", "h2"):
                    _, b, k = ev
                    hi, lo = hT(b, k)
                    v.wait_ge(mh, rd[ev] + 1)
                    fb_held[k] = use[ev] + 1
                    if kind == "h" and b == 0:
                        link(v.tensor_scalar(fb[:, 512 * k:512 * k + 512], bank(ev)[:], modt[:, 8 + 4 * k:9 + 4 * k],
                                             modt[:, 4 * k:4 * k + 1], ALU.mult, ALU.add))
                    else:
                        xv += 1
                        v.wait_ge(s_v, xv)
                    v.tensor_tensor(lo, fb[:, 512 * k:512 * k + 512], hi.bitcast(F32), ALU.subtract).then_inc(me, 1)
                elif kind in ("q", "k", "v", "z"):
                    v.wait_ge(mh, rd[ev] + 1)
                    if kind == "q":
                        hi, lo = qk[:, 0:512], qk[:, 512:1024]
                    elif kind == "k":
                        hi, lo = qk[:, 1024:1536], qk[:, 1536:2048]
                    elif kind == "v":
                        o = (ev[1] % 2) * 1024 + ev[2] * 512
                        s = slice(o, o + 512)
                        hi, lo = vh[:, s], vl[:, s]
                    else:
                        hi, lo = zs(ev[1] % 4)
                    v.tensor_tensor(lo, bank(ev)[:], hi.bitcast(F32), ALU.subtract).then_inc(me, 1)
                elif kind == "S":
                    u = ev[1]
                    if u > 0:
                        v.wait_ge(s_E, 3 * u)
                    else:
                        v.wait_ge(s_c, 16)
                    for n, (bk, chunks) in enumerate(S_ORDER):
                        v.wait_ge(s_S, 3 * u + n + 1)
                        for i in chunks:
                            a, w = S_AT[i][1], 128 * (i + 1)
                            ins = v.tensor_tensor_reduce(PS[bk][:, a:a + w], PS[bk][:, a:a + w],
                                                         mask[:, 512 - w:512], -INV, BIG, ALU.add, ALU.min,
                                                         nb[:, i:i + 1])
                        ins.then_inc(s_M, 1)
                elif kind == "norm":
                    u = ev[1]
                    v.wait_ge(s_E, 3 * u + 3)
                    if u:
                        v.wait_ge(s_P3, u)
                    v.reciprocal(ri[:], sm[:]).then_inc(s_ri, 1)
                    v.wait_ge(s_ri, u + 1)
                    for i in (1, 0, 2):
                        p = PB[:, P_OFF[i]:P_OFF[i] + 128 * (i + 1)]
                        ins = v.tensor_scalar(p, p, ri[:, i:i + 1], None, ALU.mult)
                    ins.then_inc(s_N, 1)
                elif kind == "T":
                    u = ev[1]
                    for n, (bk, _) in enumerate(T_ORDER):
                        a, z = T_COLS[bk]
                        v.wait_ge(s_ph, 3 * u + n + 1)
                        v.tensor_tensor(ptl[:, a:z], PT[bk][:, 0:z - a], pth[:, a:z].bitcast(F32),
                                        ALU.subtract).then_inc(s_pl, 1)
                elif kind == "wo":
                    _, p, c2 = ev
                    b = unit(2 * p)[1]
                    v.wait_ge(mf, use[ev] + 1)
                    if p:
                        v.wait_ge(s_y, 2 * p + c2 - 1)
                    if fb_held[c2]:
                        v.wait_ge(me, fb_held[c2])
                        fb_held[c2] = 0
                    if p == 0:
                        v.wait_ge(s_g, 16)
                    ga = gab[:, b * 256:b * 256 + 256].rearrange("p (a n) -> p a n", a=1)
                    v.tensor_tensor(fb[:, c2 * 512:c2 * 512 + 512].rearrange("p (a n) -> p a n", a=2),
                                    bank(ev)[:].rearrange("p (a n) -> p a n", a=2), bcast(ga, [128, 2, 256]),
                                    ALU.mult).then_inc(me, 1)
                elif kind in ("r", "rs"):
                    b, k = ev[1], (0 if kind == "r" else ev[2])
                    if k:
                        v.wait_ge(s_rt, 15 * b + k)
                    router(ev, b, k).then_inc(s_rt, 1)
                elif kind == "d0":
                    k = ev[1]
                    gz = g0[:, 20:180].rearrange("p (a n) -> p a n", n=8)
                    z3 = g0z[:].rearrange("p (a n) -> p a n", n=16)
                    if k == 0:
                        v.wait_ge(s_g0, 1)
                        a = g0[:, 0:20].rearrange("p (a n) -> p a n", n=1)
                        ex = cc[:, C_EXM:C_EXM + 160].rearrange("p (a n) -> p a n", n=8)
                        v.tensor_tensor(gz, ex, bcast(a, [128, 20, 8]), ALU.mult).then_inc(s_d0, 1)
                    elif k == 1:
                        v.wait_ge(s_d0, 1)
                        v.tensor_copy(z3[:, :, 0:8], gz).then_inc(s_d0, 1)
                    else:
                        v.wait_ge(s_d0, 2)
                        v.tensor_tensor(z3[:, :, 8:16], gz, z3[:, :, 0:8].bitcast(F32), ALU.subtract).then_inc(s_gz, 1)
                elif kind == "dta" and ev[1] == 2:
                    o = bank(("dt",))
                    v.wait_ge(s_dt, 1)
                    link(v.tensor_copy(g0[:, 180:188], o[:, 0:8]))
                    v.tensor_tensor(g0[:, 180:188], g0[:, 180:188], o[:, 8:16], ALU.add).then_inc(s_dc, 1)
                elif kind == "dt":
                    o = bank(ev)
                    v.wait_ge(mf, use[ev] + 1)
                    v.tensor_copy(Dm[0:8, :], o[0:8, 128:256]).then_inc(me, 1)
                elif kind == "wt":
                    v.wait_ge(mf, use[ev] + 1)
                    if ev[1] == 0:
                        v.wait_ge(s_gd, 32)
                    elif ev[1] >= 2:
                        v.wait_ge(s_ws[ev[1] - 2], 16)
                        v.wait_ge(mf, use[("D", ev[1] - 2)] + 1)
                    v.tensor_copy(wT(ev[1]), bank(ev)[0:8, :]).then_inc(me, 1)
                elif kind == "D":
                    t = ev[1]
                    if t == 0:
                        v.wait_ge(s_pa, 8)
                        v.wait_ge(mf, use[ev] + 1)
                        v.tensor_tensor(acc_at(t), acc_at(t), bank(ev)[:], ALU.add).then_inc(me, 1)
                    else:
                        v.wait_ge(mf, use[ev] + 1)
                        if t >= 2:
                            v.wait_ge(s_oc, t - 1)
                        v.tensor_scalar(acc_at(t), bank(ev)[:], bc[:, B_SH2:B_SH2 + 1], None, ALU.add).then_inc(me, 1)
                elif kind == "acc" and ev not in OWN:
                    _, t, e = ev
                    n = acc_no[(t, e)]
                    v.wait_ge(s_o, n + 1)
                    if e == 0:
                        if t == 0:
                            v.wait_ge(s_wd, 2)
                            v.tensor_scalar(acc_at(t), PT[n % 2][:], 0.1, bc[:, B_SH2:B_SH2 + 1], ALU.mult,
                                            ALU.add).then_inc(s_ac, 1)
                        else:
                            v.wait_ge(me, use[("D", t)] + 1)
                            v.scalar_tensor_tensor(out=acc_at(t), in0=PT[n % 2][:], scalar=0.1, in1=acc_at(t),
                                                   op0=ALU.mult, op1=ALU.add).then_inc(s_ac, 1)
                    else:
                        i = 8 * t + e - 1
                        v.wait_ge(s_wb[i % 4], 16 * (i // 4 + 1))
                        if i >= 2:
                            v.wait_ge(s_pa, i - 1)
                        v.tensor_tensor(prod[:, (i % 2) * 512:(i % 2) * 512 + 512], PT[n % 2][:], wb_at(i),
                                        ALU.mult).then_inc(s_ac, 1)
                elif kind == "o" and ev[1] == B - 1:
                    t, i = B - 1, 8 * B - 1
                    n = acc_no[OWN[0][1:]]
                    v.wait_ge(s_o, n + 1)
                    v.wait_ge(s_wb[i % 4], 16 * (i // 4 + 1))
                    v.wait_ge(s_pa, i)
                    v.wait_ge(mf, use[("up", t - 1, 1)] + 1)
                    for c in (0, 256):
                        q, y = prod[:, (i % 2) * 512 + c:(i % 2) * 512 + c + 256], acc_at(t)[:, c:c + 256]
                        link(v.tensor_tensor(q, PT[n % 2][:, c:c + 256], wb_at(i)[:, c:c + 256], ALU.mult))
                        link(v.tensor_tensor(y, y, q, ALU.add))
                        link(v.tensor_copy(oh[:, c:c + 256], y))
                        v.tensor_tensor(ol[:, c:c + 256], y, oh[:, c:c + 256].bitcast(F32), ALU.subtract)\
                         .then_inc(s_oc, 1)
                elif kind == "o":
                    t = ev[1]
                    if t == 0:
                        v.wait_ge(me, use[("D", t)] + 1)
                    else:
                        v.wait_ge(s_pa, 8 * t + 8)
                        v.wait_ge(mf, use[("up", t - 1, 1)] + 1)
                    link(v.tensor_copy(oh[:], acc_at(t)))
                    v.tensor_tensor(ol[:], acc_at(t), oh[:].bitcast(F32), ALU.subtract).then_inc(s_oc, 1)
                elif kind == "dn":
                    v.wait_ge(mh, rd[ev] + 1)
                    xv += 1
                    v.wait_ge(s_v, xv)
                    hi, lo = u_at(ev[1])
                    v.tensor_tensor(lo, u32(ev[1]), hi.bitcast(F32), ALU.subtract).then_inc(me, 1)
                elif kind == "gx":
                    _, t, k = ev
                    xv += 1
                    v.wait_ge(s_xg, 2 * t + k + 1)
                    v.wait_ge(s_v, xv)
                    hi, lo = gx_at(t, k)
                    v.tensor_tensor(lo, stage[:, 512:1024], hi.bitcast(F32), ALU.subtract).then_inc(s_xl, 1)
                elif kind == "w1":
                    n = ev[1]
                    xv += 1
                    v.wait_ge(s_gh, n + 1)
                    v.wait_ge(s_v, xv)
                    hi, lo = Gs(n)
                    v.tensor_tensor(lo, G32[:, (n % 2) * 512:(n % 2) * 512 + 512], hi.bitcast(F32),
                                    ALU.subtract).then_inc(s_gl, 1)
                elif kind == "up":
                    _, t, c2 = ev
                    v.wait_ge(mf, use[ev] + 1)
                    if t:
                        v.wait_ge(s_fin, 2 * t - 1 + c2)
                    fbuf = fb[:, 512 * c2:512 * c2 + 512]
                    f = fbuf.rearrange("p (a n) -> p a n", a=2)
                    g = gab[:, 1024 + t * 256:1280 + t * 256].rearrange("p (a n) -> p a n", a=1)
                    v.tensor_tensor(f, bank(ev)[:].rearrange("p (a n) -> p a n", a=2), bcast(g, [128, 2, 256]),
                                    ALU.mult).then_inc(me, 1)
                    if t == B - 1:
                        v.wait_ge(me, use[ev] + 1)
                        v.wait_ge(s_xb, 2 * t + 2)
                        y = X[:, t * 1024 + c2 * 512:t * 1024 + c2 * 512 + 512]
                        v.tensor_tensor(y, y, fbuf, ALU.add).then_inc(s_fin, 1)


def kernel(**inputs):
    import numpy as np
    import concourse.bacc as bacc
    from concourse.bass_utils import run_bass_kernel_spmd

    A = {k: np.asarray(v) for k, v in inputs.items()}
    f = "L0_ffn_"

    def rowsplit(w):
        k = w.shape[0] // 128
        return w.reshape(k, 128, -1).transpose(1, 0, 2).reshape(128, -1)

    def perhead(w):
        return w.reshape(4, 4, 128, 2, 128).transpose(0, 4, 3, 1, 2).reshape(4, 128, 1024)

    wo = A["L0_attn_W_O"].reshape(256, 4, 4, 128).transpose(1, 3, 2, 0).reshape(4, 128, 1024)
    wat = np.concatenate([perhead(A["L0_attn_W_Q"]), perhead(A["L0_attn_W_K"]), perhead(A["L0_attn_W_V"]), wo], 2)
    wfa = np.concatenate([A[f"{f}e{e}_w1"] for e in range(8)] +
                         [rowsplit(A[f + "down_w"]), rowsplit(A[f + "core_w"]), A[f + "shared_w1"],
                          A[f + "shared_w2"], A[f + "up_w"], rowsplit(A[f + "router_w"])], 1)
    wfb = np.concatenate([rowsplit(A[f"{f}e{e}_w2"]) for e in range(8)], 1)
    b1 = np.concatenate([A[f"{f}e{e}_b1"].reshape(-1, 128).T for e in range(8)], 1)
    bcol = np.concatenate([A[f + "down_b"][:, None], A[f + "shared_b1"][:, None], b1,
                           A[f + "shared_b2"][:, None]], 1)
    b2 = np.stack([A[f"{f}e{e}_b2"] for e in range(8)])
    cst = np.zeros((128, C_END), np.float32)
    cst[:, C_ID:C_ID + 128] = np.eye(128)
    cst[:, C_MASK + 384:C_MASK + 512] = np.where(np.tril(np.ones((128, 128))) > 0, 0, -1e10)
    for c, e in enumerate(EXPERT):
        cst[:, C_EXM + 8 * c:C_EXM + 8 * c + 8] = np.arange(8) != e
    cst[:, C_IOTA:C_IOTA + 8] = np.arange(8)
    cst[:, C_COST:C_COST + 8] = np.float32(1e-7) * (np.array(HID, np.float32) * 256)
    cst[:, C_ONE:C_ONE + 8] = 1
    cst[:, C_RB:C_RB + 8] = A[f + "router_b"][None]
    wm = A["L0_wmod"]
    wm = np.concatenate([wm[:, 0:768], wm[:, 1280:1536], wm[:, 768:1280]], 1)
    ins = {
        "x": rowsplit(A["L0_attn_x"].reshape(2048, 256)),
        "ct": rowsplit(np.ascontiguousarray(A["L0_c"].T)),
        "wmod": np.concatenate([rowsplit(wm[:, 0:512]), rowsplit(wm[:, 512:])], 1),
        "wat": wat, "wfa": wfa, "wfb": wfb, "cst": cst, "bcol": bcol, "b2": b2,
        "ub": A[f + "up_b"][None], "cb": A[f + "core_b"][None], 
    }
    nc = bacc.Bacc("TRN2", target_bir_lowering=False, num_devices=1)
    arrays, aps = {}, {}
    for name, a in ins.items():
        arrays["in_" + name] = np.ascontiguousarray(a)
        aps[name] = nc.dram_tensor("in_" + name, a.shape, F32, kind="ExternalInput").ap()
    out = nc.dram_tensor("out_0", (128, 4096), F32, kind="ExternalOutput").ap()
    scr = nc.dram_tensor("scr", (2, 4, 256), F32, kind="Internal").ap()
    scw = nc.dram_tensor("scw", (8 * B, 512), F32, kind="Internal").ap()
    build(nc, **aps, out=out, scr=scr, scw=scw)
    r = run_bass_kernel_spmd(nc, [arrays], core_ids=[0])
    y = np.asarray(r.results[0]["out_0"])
    return y.reshape(128, 16, 256).transpose(1, 0, 2).reshape(4, 512, 256)
```
